# Optimizing a Trainium2 kernel written in Bass

```python
import numpy as np
import jax
import jax.numpy as jnp

def _softmax(x, axis=-1):
    return jax.nn.softmax(x, axis=axis)

def _gelu(x):
    return jax.nn.gelu(x, approximate=True)

def _silu(x):
    return jax.nn.silu(x)

def _sigmoid(x):
    return jax.nn.sigmoid(x)

def _layernorm(x, axis=-1, eps=1e-05):
    m = jnp.mean(x, axis=axis, keepdims=True)
    v = jnp.var(x, axis=axis, keepdims=True)
    return (x - m) / jnp.sqrt(v + eps)

def _scatter_add(tgt, idx, src, axis=0):
    return tgt.at[idx].add(src)

def _segment_sum(src, seg, n):
    return jax.ops.segment_sum(src, seg, n)
kernel_name = 'mk_cond_seq_d2_seqx_r2_e0bc66'

def setup_inputs(seed: int=0):
    np.random.seed(seed)
    _w = jnp.asarray

    def _rec_inputs():
        import jax
        import jax.numpy as jnp
        _rk = jax.random.key(seed)
        x = -0.000125 + 0.9999 * jax.random.normal(jax.random.fold_in(_rk, 1), (2, 2048, 512), jnp.float32)
        _lenS = 2048 - jax.random.randint(jax.random.fold_in(_rk, 7), (2,), 0, max(1, 2048 // 4) + 1, jnp.int32)
        _lenS2 = 2048 - jax.random.randint(jax.random.fold_in(_rk, 8), (2,), 0, max(1, 2048 // 4) + 1, jnp.int32)
        cond_1024 = 0.00782532 + 1.00527 * jax.random.normal(jax.random.fold_in(_rk, 11), (2, 512), jnp.float32)
        return (x, cond_1024)
    x, cond_1024 = _rec_inputs()

    def _L0_cond_setup():
        import jax, jax.numpy as jnp
        import numpy as np
        D = 512
        H = 8
        WIN = 128
        DH = D // H
        EPS = 1e-05

        def _rmsnorm(x, scale):
            xf = x.astype(jnp.float32)
            var = jnp.mean(jnp.square(xf), axis=-1, keepdims=True)
            return (xf * jax.lax.rsqrt(var + EPS) * scale.astype(jnp.float32)).astype(x.dtype)

        def _rope(x):
            S, Dh = (x.shape[1], x.shape[3])
            freqs = 1.0 / 10000.0 ** (jnp.arange(0, Dh, 2, dtype=jnp.float32) / Dh)
            ang = jnp.arange(S, dtype=jnp.float32)[:, None] * freqs[None, :]
            sin = jnp.repeat(jnp.sin(ang), 2, axis=-1)[None, :, None, :]
            cos = jnp.repeat(jnp.cos(ang), 2, axis=-1)[None, :, None, :]
            x1, x2 = jnp.split(x, 2, axis=-1)
            rot = jnp.concatenate([-x2, x1], axis=-1)
            return x * cos + rot * sin
        key = jax.random.key(seed)
        ks = jax.random.split(key, 16)
        s = 0.02
        return {'group_x': jax.random.normal(ks[0], (8, 2048, D), jnp.float32), 'context': jax.random.normal(ks[1], (8, D), jnp.float32), 'W_ada': jax.random.normal(ks[2], (D, 6 * D), jnp.float32) * s, 'b_ada': jnp.zeros((6 * D,), jnp.float32), 'scale1': jnp.ones((D,), jnp.float32), 'W_qkv': jax.random.normal(ks[3], (D, 3 * D), jnp.float32) * s, 'b_qkv': jnp.zeros((3 * D,), jnp.float32), 'W_out': jax.random.normal(ks[4], (D, D), jnp.float32) * s, 'b_out': jnp.zeros((D,), jnp.float32), 'scale2': jnp.ones((D,), jnp.float32), 'W_ff1': jax.random.normal(ks[5], (D, 4 * D), jnp.float32) * s, 'b_ff1': jnp.zeros((4 * D,), jnp.float32), 'W_ff2': jax.random.normal(ks[6], (4 * D, D), jnp.float32) * s, 'b_ff2': jnp.zeros((D,), jnp.float32)}
    _L0_cond_all = _L0_cond_setup()
    _L0_cond_in = {k: v for k, v in _L0_cond_all.items() if k in ('W_ada', 'b_ada', 'scale1', 'W_qkv', 'b_qkv', 'W_out', 'b_out', 'scale2', 'W_ff1', 'b_ff1', 'W_ff2', 'b_ff2')}
    del _L0_cond_all

    def _L1_cond_setup():
        import jax, jax.numpy as jnp
        import numpy as np
        EPS = 1e-05

        def _sln(h, w, ln_g, ln_b, Wg, bg, Wb, bb):
            mu = jnp.mean(h, axis=-1, keepdims=True)
            var = jnp.mean((h - mu) ** 2, axis=-1, keepdims=True)
            ln = (h - mu) / jnp.sqrt(var + EPS) * ln_g + ln_b
            gamma = (w @ Wg.T + bg)[:, None, :]
            beta = (w @ Wb.T + bb)[:, None, :]
            return gamma * ln + beta
        key = jax.random.key(seed)
        ks = jax.random.split(key, 20)
        B, N, D = (4, 512, 512)
        F = 4 * D
        s = lambda fan: 1.0 / np.sqrt(fan)
        inp = {'hidden': jax.random.normal(ks[0], (B, N, D), jnp.float32), 'w': jax.random.normal(ks[1], (B, D), jnp.float32), 'ln_g': jnp.ones((D,), jnp.float32), 'ln_b': jnp.zeros((D,), jnp.float32), 'Wg': jax.random.normal(ks[2], (D, D), jnp.float32) * s(D), 'bg': jnp.zeros((D,), jnp.float32), 'Wb': jax.random.normal(ks[3], (D, D), jnp.float32) * s(D), 'bb': jnp.zeros((D,), jnp.float32), 'Wqkv': jax.random.normal(ks[4], (3 * D, D), jnp.float32) * s(D), 'bqkv': jnp.zeros((3 * D,), jnp.float32), 'Wp': jax.random.normal(ks[5], (D, D), jnp.float32) * s(D), 'bp': jnp.zeros((D,), jnp.float32), 'W1': jax.random.normal(ks[6], (F, D), jnp.float32) * s(D), 'b1': jnp.zeros((F,), jnp.float32), 'W2': jax.random.normal(ks[7], (D, F), jnp.float32) * s(F), 'b2': jnp.zeros((D,), jnp.float32), 'num_heads': 16}
        return inp
    _L1_cond_all = _L1_cond_setup()
    _L1_cond_in = {k: v for k, v in _L1_cond_all.items() if k in ('ln_g', 'ln_b', 'Wg', 'bg', 'Wb', 'bb', 'Wqkv', 'bqkv', 'Wp', 'bp', 'W1', 'b1', 'W2', 'b2')}
    del _L1_cond_all
    return {'x': x, 'cond_1024': cond_1024, 'L0_cond_W_ada': _L0_cond_in['W_ada'], 'L0_cond_b_ada': _L0_cond_in['b_ada'], 'L0_cond_scale1': _L0_cond_in['scale1'], 'L0_cond_W_qkv': _L0_cond_in['W_qkv'], 'L0_cond_b_qkv': _L0_cond_in['b_qkv'], 'L0_cond_W_out': _L0_cond_in['W_out'], 'L0_cond_b_out': _L0_cond_in['b_out'], 'L0_cond_scale2': _L0_cond_in['scale2'], 'L0_cond_W_ff1': _L0_cond_in['W_ff1'], 'L0_cond_b_ff1': _L0_cond_in['b_ff1'], 'L0_cond_W_ff2': _L0_cond_in['W_ff2'], 'L0_cond_b_ff2': _L0_cond_in['b_ff2'], 'L1_cond_ln_g': _L1_cond_in['ln_g'], 'L1_cond_ln_b': _L1_cond_in['ln_b'], 'L1_cond_Wg': _L1_cond_in['Wg'], 'L1_cond_bg': _L1_cond_in['bg'], 'L1_cond_Wb': _L1_cond_in['Wb'], 'L1_cond_bb': _L1_cond_in['bb'], 'L1_cond_Wqkv': _L1_cond_in['Wqkv'], 'L1_cond_bqkv': _L1_cond_in['bqkv'], 'L1_cond_Wp': _L1_cond_in['Wp'], 'L1_cond_bp': _L1_cond_in['bp'], 'L1_cond_W1': _L1_cond_in['W1'], 'L1_cond_b1': _L1_cond_in['b1'], 'L1_cond_W2': _L1_cond_in['W2'], 'L1_cond_b2': _L1_cond_in['b2']}

def reference(x, cond_1024, L0_cond_W_ada, L0_cond_b_ada, L0_cond_scale1, L0_cond_W_qkv, L0_cond_b_qkv, L0_cond_W_out, L0_cond_b_out, L0_cond_scale2, L0_cond_W_ff1, L0_cond_b_ff1, L0_cond_W_ff2, L0_cond_b_ff2, L1_cond_ln_g, L1_cond_ln_b, L1_cond_Wg, L1_cond_bg, L1_cond_Wb, L1_cond_bb, L1_cond_Wqkv, L1_cond_bqkv, L1_cond_Wp, L1_cond_bp, L1_cond_W1, L1_cond_b1, L1_cond_W2, L1_cond_b2):
    import jax
    import jax.numpy as jnp

    def _L0_cond_ref(group_x, context, W_ada, b_ada, scale1, W_qkv, b_qkv, W_out, b_out, scale2, W_ff1, b_ff1, W_ff2, b_ff2):
        import jax, jax.numpy as jnp
        import numpy as np
        D = 512
        H = 8
        WIN = 128
        DH = D // H
        EPS = 1e-05

        def _rmsnorm(x, scale):
            xf = x.astype(jnp.float32)
            var = jnp.mean(jnp.square(xf), axis=-1, keepdims=True)
            return (xf * jax.lax.rsqrt(var + EPS) * scale.astype(jnp.float32)).astype(x.dtype)

        def _rope(x):
            S, Dh = (x.shape[1], x.shape[3])
            freqs = 1.0 / 10000.0 ** (jnp.arange(0, Dh, 2, dtype=jnp.float32) / Dh)
            ang = jnp.arange(S, dtype=jnp.float32)[:, None] * freqs[None, :]
            sin = jnp.repeat(jnp.sin(ang), 2, axis=-1)[None, :, None, :]
            cos = jnp.repeat(jnp.cos(ang), 2, axis=-1)[None, :, None, :]
            x1, x2 = jnp.split(x, 2, axis=-1)
            rot = jnp.concatenate([-x2, x1], axis=-1)
            return x * cos + rot * sin
        B, L, _ = group_x.shape
        nw = L // WIN
        ada = jax.nn.silu(context) @ W_ada + b_ada
        sh_msa, sc_msa, g_msa, sh_mlp, sc_mlp, g_mlp = jnp.split(ada, 6, axis=-1)
        sh_msa, sc_msa, g_msa = (sh_msa[:, None], sc_msa[:, None], g_msa[:, None])
        sh_mlp, sc_mlp, g_mlp = (sh_mlp[:, None], sc_mlp[:, None], g_mlp[:, None])
        res = group_x
        x = _rmsnorm(group_x, scale1)
        x = x * (1 + sc_msa) + sh_msa
        xw = x.reshape(B * nw, WIN, D)
        qkv = xw @ W_qkv + b_qkv
        q, k, v = jnp.split(qkv, 3, axis=-1)
        q = _rope(q.reshape(B * nw, WIN, H, DH))
        k = _rope(k.reshape(B * nw, WIN, H, DH))
        v = v.reshape(B * nw, WIN, H, DH)
        scores = jnp.einsum('bqhd,bkhd->bhqk', q, k) / jnp.sqrt(jnp.float32(DH))
        attn = jax.nn.softmax(scores, axis=-1)
        o = jnp.einsum('bhqk,bkhd->bqhd', attn, v).reshape(B, L, D)
        o = o @ W_out + b_out
        x = res + g_msa * o
        res = x
        h = _rmsnorm(x, scale2)
        h = h * (1 + sc_mlp) + sh_mlp
        h = jax.nn.gelu(h @ W_ff1 + b_ff1)
        h = h @ W_ff2 + b_ff2
        return res + g_mlp * h

    def _L1_cond_ref(hidden, w, ln_g, ln_b, Wg, bg, Wb, bb, Wqkv, bqkv, Wp, bp, W1, b1, W2, b2, num_heads):
        import jax, jax.numpy as jnp
        import numpy as np
        EPS = 1e-05

        def _sln(h, w, ln_g, ln_b, Wg, bg, Wb, bb):
            mu = jnp.mean(h, axis=-1, keepdims=True)
            var = jnp.mean((h - mu) ** 2, axis=-1, keepdims=True)
            ln = (h - mu) / jnp.sqrt(var + EPS) * ln_g + ln_b
            gamma = (w @ Wg.T + bg)[:, None, :]
            beta = (w @ Wb.T + bb)[:, None, :]
            return gamma * ln + beta
        B, N, D = hidden.shape
        hd = D // num_heads
        h = _sln(hidden, w, ln_g, ln_b, Wg, bg, Wb, bb)
        qkv = (h @ Wqkv.T + bqkv).reshape(B, N, num_heads, hd, 3)
        q = jnp.moveaxis(qkv[..., 0], 2, 1)
        k = jnp.moveaxis(qkv[..., 1], 2, 1)
        v = jnp.moveaxis(qkv[..., 2], 2, 1)
        energy = jnp.einsum('bhqd,bhkd->bhqk', q, k)
        att = jax.nn.softmax(energy, axis=-1) / D ** 0.5
        out = jnp.einsum('bhqk,bhkd->bhqd', att, v)
        out = jnp.moveaxis(out, 1, 2).reshape(B, N, D)
        out = out @ Wp.T + bp
        h1 = out + hidden
        h2 = _sln(h1, w, ln_g, ln_b, Wg, bg, Wb, bb)
        return h2 + h1
    x = _L0_cond_ref(x, cond_1024, L0_cond_W_ada, L0_cond_b_ada, L0_cond_scale1, L0_cond_W_qkv, L0_cond_b_qkv, L0_cond_W_out, L0_cond_b_out, L0_cond_scale2, L0_cond_W_ff1, L0_cond_b_ff1, L0_cond_W_ff2, L0_cond_b_ff2)
    x = _L1_cond_ref(x, cond_1024, L1_cond_ln_g, L1_cond_ln_b, L1_cond_Wg, L1_cond_bg, L1_cond_Wb, L1_cond_bb, L1_cond_Wqkv, L1_cond_bqkv, L1_cond_Wp, L1_cond_bp, L1_cond_W1, L1_cond_b1, L1_cond_W2, L1_cond_b2, 16)
    return x

_drawn_inputs = setup_inputs


def setup_inputs(seed=0):
    import zlib

    import numpy as np

    out = dict(_drawn_inputs(seed))
    spreads = {'L0_cond_b_ada': (0.0, 0.297),
     'L0_cond_scale1': (1.0, 0.6),
     'L0_cond_b_qkv': (0.0, 0.8),
     'L0_cond_b_out': (0.0, 0.326),
     'L0_cond_scale2': (1.0, 0.6),
     'L0_cond_b_ff1': (0.0, 0.661),
     'L0_cond_b_ff2': (0.0, 0.362),
     'L1_cond_ln_g': (1.0, 0.2),
     'L1_cond_ln_b': (0.0, 0.1),
     'L1_cond_bg': (0.0, 0.1),
     'L1_cond_bb': (0.0, 0.1),
     'L1_cond_bqkv': (0.0, 2.0),
     'L1_cond_bp': (0.0, 0.1),
     'L1_cond_b1': (0.0, 0.1),
     'L1_cond_b2': (0.0, 0.1)}
    factors = {'L0_cond_W_qkv': 3.547, 'L0_cond_W_out': 3.401}
    for name, (base, spread) in spreads.items():
        noise = np.random.default_rng([zlib.crc32(name.encode()), seed]).standard_normal(out[name].shape)
        drawn = base * np.exp(spread * noise) if base else spread * noise
        out[name] = jnp.asarray(drawn.astype(out[name].dtype))
    for name, factor in factors.items():
        out[name] = (out[name] * factor).astype(out[name].dtype)
    return out
```

```python
from contextlib import ExitStack

import concourse.bass as bass
from concourse import mybir

F32 = mybir.dt.float32
F32R = mybir.dt.float32r
ALU = mybir.AluOpType
ACT = mybir.ActivationFunctionType
AX = mybir.AxisListType
ds = bass.ds

P = 128
D = 512
C = D // P
EPS = 1e-5

SCALE0, SHIFT0, SCALE1, SHIFT1, SCALE2, SHIFT2, GATE0, GBIAS0, GATE1, GBIAS1 = range(10)
MODS = 10
COLS = 6


def wait(eng, sem, value):
    if not isinstance(value, int) or value > 0:
        eng.wait_ge(sem, value)


def live(index, count):
    return not isinstance(index, int) or 0 <= index < count


def back(j, u, lag):
    t = u - lag
    return 2 * j + t, t % 2, j + t // 2


def pipeline(eng, steps, head, tail, step):
    for s in range(head):
        step(*divmod(s, 2))
    with eng.Fori(head // 2, (steps - tail) // 2) as j:
        for u in range(2):
            step(j, u)
    for s in range(steps - tail, steps):
        step(*divmod(s, 2))


def triple(pe, out, lhs, rhs, start, stop):
    pe.matmul(out, lhs[1], rhs[0], start=start, stop=False)
    pe.matmul(out, lhs[0], rhs[1], start=False, stop=False)
    return pe.matmul(out, lhs[0], rhs[0], start=False, stop=stop)


class Memory:

    def __init__(self, nc, stack, phase):
        self.nc, self.stack, self.phase = nc, stack, phase
        self.sems = []

    def sb(self, name, shape, dt=F32):
        return self.stack.enter_context(self.nc.sbuf_tensor(f"{self.phase}_{name}", shape, dt))

    def ps(self, name, shape, dt=F32):
        return self.stack.enter_context(self.nc.psum_tensor(f"{self.phase}_{name}", shape, dt))

    def sem(self, name):
        self.sems.append(self.stack.enter_context(self.nc.semaphore(f"{self.phase}_{name}")))
        return self.sems[-1]

    def clear(self):
        with self.nc.Block() as block:
            @block.gpsimd
            def _(pool):
                for sem in self.sems:
                    pool.sem_clear(sem)


class Weights:

    def __init__(self, mem, chunks):
        self.chunks = chunks
        self.stage = [mem.sb(f"wstage{n}", [P, 2048]) for n in range(2)]
        self.loaded = [mem.sem(f"w_loaded{n}") for n in range(2)]
        self.hi_done = mem.sem("w_hi_done")
        self.lo_done = mem.sem("w_lo_done")

    def staged(self, n):
        a = self.chunks[n][0].shape[1]
        return self.stage[n % 2][:].rearrange("p (a b) -> p a b", a=a)

    def load(self, sp):
        for n, (source, _, _) in enumerate(self.chunks):
            wait(sp, self.lo_done, n - 1)
            sp.dma_start(self.staged(n), source).then_inc(self.loaded[n % 2], 16)

    def round_hi(self, act):
        for n, (_, hi, _) in enumerate(self.chunks):
            act.wait_ge(self.loaded[n % 2], 16 * (n // 2 + 1))
            act.activation(hi, self.staged(n), ACT.Copy).then_inc(self.hi_done, 1)

    def rest_lo(self, dve):
        for n, (_, hi, lo) in enumerate(self.chunks):
            dve.wait_ge(self.hi_done, n + 1)
            dve.tensor_tensor(lo, self.staged(n), hi.bitcast(F32), ALU.subtract).then_inc(self.lo_done, 1)

    def wait_split(self, pe):
        pe.wait_ge(self.lo_done, len(self.chunks))


def modulation(nc, dram, mods, ident, cols):
    with ExitStack() as stack:
        m = Memory(nc, stack, "mod")
        B = 2
        VEC = ["scale1", "scale2", "b_out", "b_ff2", "ln_g", "ln_b"]
        cond_rows = m.sb("cond_rows", [B * C, P])
        cond = m.sb("cond", [P, B, C])
        sig = m.sb("sig", [P, B, C])
        silu = m.sb("silu", [P, B, C])
        w_ada = m.sb("w_ada", [P, C, 6 * D])
        w_style = m.sb("w_style", [P, C, 2, D])
        bias = m.sb("bias", [B, 8, D])
        vec = m.sb("vec", [B, len(VEC), D])
        raw = m.sb("raw", [B, 8, D])
        made = m.sb("made", [B, 6, D])
        rows = m.sb("rows", [72, P])
        ps = m.ps("ps", [P, 8, D])
        cond_loaded, vec_loaded, ada_loaded, style_loaded = (m.sem(x) for x in (
            "cond_loaded", "vec_loaded", "ada_loaded", "style_loaded"))
        cond_mm, cond_done = m.sem("cond_mm"), m.sem("cond_done")
        exp_done, sig_done, silu_done, raw_mm, raw_done, made_done = (m.sem(x) for x in (
            "exp_done", "sig_done", "silu_done", "raw_mm", "raw_done", "made_done"))
        table_stored, rows_loaded, cols_mm, cols_done = (m.sem(x) for x in (
            "table_stored", "rows_loaded", "cols_mm", "cols_done"))
        inner = stack.enter_context(ExitStack())
        block = inner.enter_context(nc.Block())

        MADE = [SCALE0, SCALE1, SCALE2, SHIFT2, GBIAS0, GBIAS1]
        RAW = {SHIFT0: 0, GATE0: 2, SHIFT1: 3, GATE1: 5}

        @block.sync
        def _(sp):
            sp.dma_start(cond_rows[:], dram["cond"].rearrange("b (c p) -> (b c) p", p=P)).then_inc(cond_loaded, 16)
            sp.dma_start(ident[:], dram["ident"]).then_inc(cond_loaded, 16)
            for n in range(6):
                sp.dma_start(w_ada[:, :, n * D:(n + 1) * D],
                             dram["w_ada"].rearrange("(c p) n -> p c n", p=P)[:, :, n * D:(n + 1) * D]
                             ).then_inc(ada_loaded, 16)
            sp.dma_start(bias[:, 0:6, :].rearrange("b n d -> b (n d)"),
                         dram["b_ada"].partition_broadcast(B)).then_inc(vec_loaded, 16)
            sp.dma_start(bias[:, 6, :], dram["bg"].partition_broadcast(B)).then_inc(vec_loaded, 16)
            sp.dma_start(bias[:, 7, :], dram["bb"].partition_broadcast(B)).then_inc(vec_loaded, 16)
            for n, name in enumerate(VEC):
                sp.dma_start(vec[:, n, :], dram[name].partition_broadcast(B)).then_inc(vec_loaded, 16)
            sp.dma_start(w_style[:, :, 0, :], dram["wg_t"].rearrange("(c p) n -> p c n", p=P)).then_inc(style_loaded, 16)
            sp.dma_start(w_style[:, :, 1, :], dram["wb_t"].rearrange("(c p) n -> p c n", p=P)).then_inc(style_loaded, 16)
            sp.wait_ge(raw_done, 1)
            for row, n in RAW.items():
                sp.dma_start(mods[:, row, :], raw[:, n, :]).then_inc(table_stored, 16)
            sp.wait_ge(made_done, 7)
            for n, row in enumerate(MADE):
                sp.dma_start(mods[:, row, :], made[:, n, :]).then_inc(table_stored, 16)
            sp.wait_ge(table_stored, 160)
            for b in range(B):
                sp.dma_start(rows[24 * b:24 * b + 24, :],
                             mods[b, 0:COLS, :].rearrange("v (c p) -> (v c) p", p=P)).then_inc(rows_loaded, 16)
            sp.dma_start(rows[48:64, :], dram["b_ff1"].rearrange("(c p) -> c p", p=P)).then_inc(rows_loaded, 16)
            sp.dma_start(rows[64:68, :], dram["b_q1"].rearrange("(c p) -> c p", p=P)).then_inc(rows_loaded, 16)
            sp.dma_start(rows[68:72, :], dram["b_k1"].rearrange("(c p) -> c p", p=P)).then_inc(rows_loaded, 16)

        @block.scalar
        def _(act):
            act.wait_ge(cond_done, 1)
            act.activation(sig[:], cond[:], ACT.Exp, scale=-1.0).then_inc(exp_done, 1)

        @block.vector
        def _(dve):
            dve.wait_ge(cond_mm, 1)
            dve.tensor_copy(cond[:].rearrange("p b c -> p (b c)"), ps[:, 0, 0:B * C]).then_inc(cond_done, 1)
            dve.wait_ge(exp_done, 1)
            dve.tensor_scalar(sig[:], sig[:], 1.0, None, ALU.add).then_inc(sig_done, 1)
            dve.wait_ge(sig_done, 1)
            dve.reciprocal(sig[:], sig[:]).then_inc(sig_done, 1)
            dve.wait_ge(sig_done, 2)
            dve.tensor_tensor(silu[:], cond[:], sig[:], ALU.mult).then_inc(silu_done, 1)
            dve.wait_ge(raw_mm, 1)
            dve.wait_ge(vec_loaded, 144)
            dve.tensor_tensor(raw[:], ps[0:B], bias[:], ALU.add).then_inc(raw_done, 1)
            dve.wait_ge(raw_done, 1)
            dve.scalar_tensor_tensor(made[:, 0, :], raw[:, 1, :], 1.0, vec[:, 0, :], ALU.add, ALU.mult).then_inc(made_done, 1)
            dve.scalar_tensor_tensor(made[:, 1, :], raw[:, 4, :], 1.0, vec[:, 1, :], ALU.add, ALU.mult).then_inc(made_done, 1)
            dve.tensor_tensor(made[:, 2, :], raw[:, 6, :], vec[:, 4, :], ALU.mult).then_inc(made_done, 1)
            dve.tensor_tensor(made[:, 3, :], raw[:, 6, :], vec[:, 5, :], ALU.mult).then_inc(made_done, 1)
            dve.tensor_tensor(made[:, 4, :], raw[:, 2, :], vec[:, 2, :], ALU.mult).then_inc(made_done, 1)
            dve.tensor_tensor(made[:, 5, :], raw[:, 5, :], vec[:, 3, :], ALU.mult).then_inc(made_done, 1)
            dve.wait_ge(made_done, 6)
            dve.tensor_tensor(made[:, 3, :], made[:, 3, :], raw[:, 7, :], ALU.add).then_inc(made_done, 1)
            dve.wait_ge(cols_mm, 1)
            dve.tensor_copy(cols[:], ps[:, 0, 0:72]).then_inc(cols_done, 1)
            dve.wait_ge(cols_done, 1)

        @block.tensor
        def _(pe):
            pe.wait_ge(cond_loaded, 32)
            pe.transpose(ps[:, 0, 0:B * C], cond_rows[:], ident[0:B * C, 0:B * C]).then_inc(cond_mm, 1)
            pe.wait_ge(silu_done, 1)
            for n in range(8):
                if n == 6:
                    pe.wait_ge(style_loaded, 32)
                elif n < 6:
                    pe.wait_ge(ada_loaded, 96)
                for c in range(C):
                    lhs = silu[:, :, c] if n < 6 else cond[:, :, c]
                    rhs = w_ada[:, c, n * D:(n + 1) * D] if n < 6 else w_style[:, c, n - 6, :]
                    mm = pe.matmul(ps[0:B, n, :], lhs, rhs, start=c == 0, stop=c == C - 1)
            mm.then_inc(raw_mm, 1)
            pe.wait_ge(rows_loaded, 80)
            pe.wait_ge(raw_done, 1)
            pe.transpose(ps[:, 0, 0:72], rows[:], ident[0:72, 0:72]).then_inc(cols_mm, 1)

        inner.close()
        m.clear()


def column(cols, row, b, c):
    return cols[:, ds(b * (COLS * C) + (row * C + c), 1)]


def window_attention(nc, dram, x, x1, mods, ident, cols, T):
    N = T // P
    WPB = N // 2
    H, DH = 8, 64
    with ExitStack() as stack:
        m = Memory(nc, stack, "win")
        wqkv = [m.sb(f"wqkv{n}", [P, C, 3 * D], F32R) for n in range(2)]
        wout = [m.sb(f"wout{n}", [P, C, D], F32R) for n in range(2)]
        wq_src = dram["w_qkv0"].rearrange("(c p) n -> p c n", p=P)
        weights = Weights(m, [(wq_src[:, :, n * D:(n + 1) * D], *(w[:, :, n * D:(n + 1) * D] for w in wqkv)) for n in range(3)]
                          + [(dram["w_out0"].rearrange("(c p) n -> p c n", p=P), *(w[:] for w in wout))])
        bqkv = m.sb("bqkv", [P, 3, D])
        gate = m.sb("gate", [P, 2, D])
        gbias = m.sb("gbias", [P, 2, D])
        cos = m.sb("cos", [P, DH])
        sin = m.sb("sin", [P, DH])
        xw = m.sb("xw", [P, 2, D])
        sq = m.sb("sq", [P, D])
        ss = m.sb("ss", [P, 2])
        var = m.sb("var", [P, 2])
        half = m.sb("half", [P, 1])
        eps = m.sb("eps", [P, 1])
        rstd = m.sb("rstd", [P, 2])
        xn = m.sb("xn", [P, 2, D])
        hf = m.sb("hf", [P, C, P])
        hh = m.sb("hh", [P, 2, C, P], F32R)
        hl = m.sb("hl", [P, 2, C, P], F32R)
        qk = m.sb("qk", [P, 2 * D])
        rot = m.sb("rot", [P, 2 * D])
        qkr = m.sb("qkr", [P, 2 * D])
        v = m.sb("v", [P, 2, D])
        qkt = m.sb("qkt", [P, 2, C, P])
        negmax = m.sb("negmax", [P, H])
        pr = m.sb("pr", [P, H, P])
        sums = m.sb("sums", [P, H])
        rsum = m.sb("rsum", [P, H])
        prt = m.sb("prt", [P, H, P])
        o = m.sb("o", [P, D])
        oh = m.sb("oh", [P, C, P], F32R)
        ol = m.sb("ol", [P, C, P], F32R)
        gated = m.sb("gated", [P, D])
        xres = m.sb("xres", [P, 2, D])
        xo = m.sb("xo", [P, 2, D])
        ps_x = m.ps("ps_x", [P, D])
        ps_mm = m.ps("ps_mm", [P, 2, D])
        ps_t = m.ps("ps_t", [P, 2, D])
        ps_s = m.ps("ps_s", [P, 2, D])
        s = m.sem
        const_loaded, pow_set = s("const_loaded"), s("pow_set")
        x_loaded, xres_loaded, stored = ([s(f"{n}{i}") for i in range(2)] for n in ("x_loaded", "xres_loaded", "stored"))
        sq_done, var_done, rstd_done, xn_done = s("sq_done"), s("var_done"), s("rstd_done"), s("xn_done")
        xt_mm, affine_done, hh_done, hl_done = s("xt_mm"), s("affine_done"), s("hh_done"), s("hl_done")
        qkv_mm, qkv_out, rope_part, rope_done = s("qkv_mm"), s("qkv_out"), s("rope_part"), s("rope_done")
        qkt_mm, qkt_out, score_mm, max_done, exp_done = s("qkt_mm"), s("qkt_out"), s("score_mm"), s("max_done"), s("exp_done")
        prt_mm, prt_out, pv_mm, rsum_done, o_done = s("prt_mm"), s("prt_out"), s("pv_mm"), s("rsum_done"), s("o_done")
        ot_mm, oh_done, ol_done, out_mm, gated_done, xres_done, x1_done = (s(n) for n in (
            "ot_mm", "oh_done", "ol_done", "out_mm", "gated_done", "xres_done", "x1_done"))
        block = stack.enter_context(nc.Block())

        STEPS, HEAD, TAIL = N + 4, 4, 4

        def score(h):
            return ps_s[:, h % 2, (h // 2) * P:(h // 2 + 1) * P]

        @block.sync
        def _(sp):
            weights.load(sp)
            sp.dma_start(cos[:], dram["cos"]).then_inc(const_loaded, 16)
            sp.dma_start(sin[:], dram["sin"]).then_inc(const_loaded, 16)
            sp.dma_start(bqkv[:].rearrange("p a b -> p (a b)"), dram["b_qkv0"].partition_broadcast(P)).then_inc(const_loaded, 16)
            for b in range(2):
                sp.dma_start(gate[:, b], mods[b, GATE0].partition_broadcast(P)).then_inc(const_loaded, 16)
                sp.dma_start(gbias[:, b], mods[b, GBIAS0].partition_broadcast(P)).then_inc(const_loaded, 16)

            def step(j, u):
                w, p, _ = back(j, u, 4)
                if live(w, N):
                    wait(sp, x1_done, w + 1)
                    sp.dma_start(x1[ds(w * P, P), :], xo[:, p]).then_inc(stored[p], 16)
                w, p, _ = back(j, u, 3)
                if live(w, N):
                    wait(sp, x1_done, w - 1)
                    sp.dma_start(xres[:, p], x[ds(w * P, P), :]).then_inc(xres_loaded[p], 16)
                w, p, _ = back(j, u, 0)
                if live(w, N):
                    wait(sp, xn_done, w - 1)
                    sp.dma_start(xw[:, p], x[ds(w * P, P), :]).then_inc(x_loaded[p], 16)

            pipeline(sp, STEPS, HEAD, TAIL, step)
            for p in range(2):
                sp.wait_ge(stored[p], 16 * (N // 2))

        @block.gpsimd
        def _(pool):
            pool.memset(half[:], -0.5).then_inc(pow_set, 1)
            pool.memset(eps[:], EPS).then_inc(pow_set, 1)
            pool.wait_ge(pow_set, 2)
            pool.wait_ge(const_loaded, 112)

            def step(j, u):
                w, p, _ = back(j, u, 0)
                if live(w, N):
                    wait(pool, sq_done, w + 1)
                    pool.tensor_tensor(var[:, p:p + 1], ss[:, p:p + 1], eps[:], ALU.add).then_inc(var_done, 1)
                    wait(pool, var_done, w + 1)
                    pool.tensor_tensor(rstd[:, p:p + 1], var[:, p:p + 1], half[:], ALU.pow).then_inc(rstd_done, 1)
                w, p, k = back(j, u, 3)
                if live(w, N):
                    wait(pool, xres_loaded[p], 16 * (k + 1))
                    pool.tensor_tensor(xres[:, p], xres[:, p], gbias[:, ds(w // WPB, 1), :].rearrange("p a d -> p (a d)"),
                                       ALU.add).then_inc(xres_done, 1)

            pipeline(pool, STEPS, HEAD, TAIL, step)

        @block.scalar
        def _(act):
            weights.round_hi(act)

            def step(j, u):
                w, p, _ = back(j, u, 2)
                if live(w, N):
                    for i in range(2):
                        wait(act, qkt_mm, 2 * w + 1 + i)
                        if i == 0:
                            wait(act, score_mm, w)
                        act.activation(qkt[:, i], ps_t[:, i, :].rearrange("p (c t) -> p c t", c=C), ACT.Copy,
                                       scale=0.125 if i == 0 else 1.0).then_inc(qkt_out, 1)
                w3, _, _ = back(j, u, 3)
                if live(w3, N):
                    wait(act, ot_mm, w3 + 1)
                    wait(act, out_mm, w3)
                    act.activation(oh[:], ps_s[:, 1, :].rearrange("p (c t) -> p c t", c=C), ACT.Copy).then_inc(oh_done, 1)
                w0, p0, k0 = back(j, u, 0)
                if live(w0, N):
                    wait(act, x_loaded[p0], 16 * (k0 + 1))
                    act.activation(sq[:], xw[:, p0], ACT.Square, scale=D ** -0.5, accum_out=ss[:, p0:p0 + 1]).then_inc(sq_done, 1)
                if live(w, N):
                    wait(act, max_done, w + 1)
                    for h in range(H):
                        e = act.activation(pr[:, h], score(h), ACT.Exp, bias=negmax[:, 4 * (h % 2) + h // 2:4 * (h % 2) + h // 2 + 1],
                                           accum_out=sums[:, h:h + 1])
                    e.then_inc(exp_done, 1)
                    for i in range(2):
                        wait(act, prt_mm, 2 * w + 1 + i)
                        if i == 0:
                            wait(act, pv_mm, w)
                        act.activation(prt[:, 4 * i:4 * i + 4], ps_t[:, i, :].rearrange("p (h t) -> p h t", h=4),
                                       ACT.Copy).then_inc(prt_out, 1)
                if live(w0, N):
                    wait(act, xt_mm, w0 + 1)
                    wait(act, hl_done, w0)
                    for c in range(C):
                        a = act.activation(hf[:, c], ps_x[:, c * P:(c + 1) * P], ACT.Identity,
                                           scale=column(cols, SCALE0, w0 // WPB, c), bias=column(cols, SHIFT0, w0 // WPB, c))
                    a.then_inc(affine_done, 1)

            pipeline(act, STEPS, HEAD, TAIL, step)

        @block.vector
        def _(dve):
            weights.rest_lo(dve)
            dve.wait_ge(const_loaded, 112)
            qk_h = qk[:].rearrange("p (h z d) -> p h z d", z=2, d=DH // 2)
            rot_h = rot[:].rearrange("p (h z d) -> p h z d", z=2, d=DH // 2)

            def step(j, u):
                w1, p1, _ = back(j, u, 1)
                w2, p2, _ = back(j, u, 2)
                w0, p0, _ = back(j, u, 0)
                w3, p3, k3 = back(j, u, 3)
                if live(w3, N):
                    wait(dve, oh_done, w3 + 1)
                    dve.tensor_tensor(ol[:], ps_s[:, 1, :].rearrange("p (c t) -> p c t", c=C), oh[:].bitcast(F32),
                                      ALU.subtract).then_inc(ol_done, 1)
                if live(w1, N):
                    wait(dve, qkv_mm, 3 * w1 + 1)
                    wait(dve, rope_done, w1)
                    dve.tensor_tensor(qk[:, 0:D], ps_mm[:, 0, :], bqkv[:, 0, :], ALU.add).then_inc(qkv_out, 1)
                if live(w2, N):
                    wait(dve, score_mm, w2 + 1)
                    dve.tensor_reduce(negmax[:], ps_s[:].rearrange("p a (h k) -> p (a h) k", k=P), AX.X, ALU.max,
                                      negate=True).then_inc(max_done, 1)
                if live(w1, N):
                    wait(dve, qkv_mm, 3 * w1 + 2)
                    dve.tensor_tensor(qk[:, D:2 * D], ps_mm[:, 1, :], bqkv[:, 1, :], ALU.add).then_inc(qkv_out, 1)
                if live(w0, N):
                    wait(dve, rstd_done, w0 + 1)
                    wait(dve, xt_mm, w0 - 1)
                    dve.tensor_scalar(xn[:, p0], xw[:, p0], rstd[:, p0:p0 + 1], None, ALU.mult).then_inc(xn_done, 1)
                if live(w1, N):
                    wait(dve, qkt_mm, 2 * w1)
                    wait(dve, qkv_out, 3 * w1 + 2)
                    dve.tensor_tensor(rot_h[:, :, 0, :], qk_h[:, :, 1, :],
                                      sin[:, 0:32].unsqueeze(1).to_broadcast([P, 16, 32]), ALU.mult).then_inc(rope_part, 1)
                    dve.tensor_tensor(rot_h[:, :, 1, :], qk_h[:, :, 0, :],
                                      sin[:, 32:64].unsqueeze(1).to_broadcast([P, 16, 32]), ALU.mult).then_inc(rope_part, 1)
                    dve.tensor_tensor(qkr[:].rearrange("p (h d) -> p h d", d=DH), qk[:].rearrange("p (h d) -> p h d", d=DH),
                                      cos[:].unsqueeze(1).to_broadcast([P, 16, DH]), ALU.mult).then_inc(rope_part, 1)
                    wait(dve, qkv_mm, 3 * w1 + 3)
                    wait(dve, pv_mm, w1 - 1)
                    dve.tensor_tensor(v[:, p1], ps_mm[:, 0, :], bqkv[:, 2, :], ALU.add).then_inc(qkv_out, 1)
                    wait(dve, rope_part, 3 * w1 + 3)
                    dve.tensor_tensor(qkr[:], qkr[:], rot[:], ALU.add).then_inc(rope_done, 1)
                if live(w2, N):
                    wait(dve, exp_done, w2 + 1)
                    dve.reciprocal(rsum[:], sums[:]).then_inc(rsum_done, 1)
                if live(w0, N):
                    wait(dve, affine_done, w0 + 1)
                    dve.tensor_copy(hh[:, p0], hf[:]).then_inc(hh_done, 1)
                    wait(dve, hh_done, w0 + 1)
                    dve.tensor_tensor(hl[:, p0], hf[:], hh[:, p0].bitcast(F32), ALU.subtract).then_inc(hl_done, 1)
                if live(w3, N):
                    wait(dve, out_mm, w3 + 1)
                    dve.tensor_tensor(gated[:], ps_mm[:, 1, :], gate[:, ds(w3 // WPB, 1), :].rearrange("p a d -> p (a d)"),
                                      ALU.mult).then_inc(gated_done, 1)
                if live(w2, N):
                    wait(dve, pv_mm, w2 + 1)
                    wait(dve, rsum_done, w2 + 1)
                    dve.tensor_tensor(o[:].rearrange("p (h d) -> p h d", d=DH), ps_s[:, 0, :].rearrange("p (h d) -> p h d", d=DH),
                                      rsum[:].unsqueeze(2).to_broadcast([P, H, DH]), ALU.mult).then_inc(o_done, 1)
                if live(w3, N):
                    wait(dve, gated_done, w3 + 1)
                    wait(dve, xres_done, w3 + 1)
                    wait(dve, stored[p3], 16 * k3)
                    dve.tensor_tensor(xo[:, p3], gated[:], xres[:, p3], ALU.add).then_inc(x1_done, 1)

            pipeline(dve, STEPS, HEAD, TAIL, step)

        @block.tensor
        def _(pe):
            weights.wait_split(pe)

            def project(w, p, n):
                for c in range(C):
                    mm = triple(pe, ps_mm[:, n % 2, :], (hh[:, p, c, :], hl[:, p, c, :]),
                                [x_[:, c, n * D:(n + 1) * D] for x_ in wqkv], c == 0, c == C - 1)
                mm.then_inc(qkv_mm, 1)

            def step(j, u):
                w0, p0, _ = back(j, u, 0)
                w1, p1, _ = back(j, u, 1)
                w2, p2, _ = back(j, u, 2)
                w3, p3, _ = back(j, u, 3)
                if live(w2, N):
                    wait(pe, rope_done, w2 + 1)
                    wait(pe, prt_out, 2 * w2)
                    for i in range(2):
                        for c in range(C):
                            mm = pe.transpose(ps_t[:, i, c * P:(c + 1) * P], qkr[:, i * D + c * P:i * D + (c + 1) * P], ident[:])
                        mm.then_inc(qkt_mm, 1)
                if live(w3, N):
                    wait(pe, o_done, w3 + 1)
                    for c in range(C):
                        mm = pe.transpose(ps_s[:, 1, c * P:(c + 1) * P], o[:, c * P:(c + 1) * P], ident[:])
                    mm.then_inc(ot_mm, 1)
                if live(w1, N):
                    wait(pe, hl_done, w1 + 1)
                    wait(pe, qkv_out, 3 * w1)
                    project(w1, p1, 0)
                if live(w2, N):
                    wait(pe, qkt_out, 2 * w2 + 2)
                    wait(pe, o_done, w2)
                    wait(pe, ol_done, w2)
                    for h in range(H):
                        at = slice(64 * (h % 2), 64 * (h % 2) + 64)
                        mm = pe.matmul(score(h), qkt[at, 0, h // 2, :], qkt[at, 1, h // 2, :],
                                       start=True, stop=True)
                    mm.then_inc(score_mm, 1)
                if live(w1, N):
                    wait(pe, gated_done, w1 - 2)
                    project(w1, p1, 1)
                    wait(pe, qkv_out, 3 * w1 + 1)
                    project(w1, p1, 2)
                if live(w2, N):
                    wait(pe, exp_done, w2 + 1)
                    for h in range(H):
                        mm = pe.transpose(ps_t[:, h // 4, (h % 4) * P:(h % 4 + 1) * P], pr[:, h, :], ident[:])
                        if h % 4 == 3:
                            mm.then_inc(prt_mm, 1)
                if live(w0, N):
                    wait(pe, xn_done, w0 + 1)
                    wait(pe, affine_done, w0)
                    for c in range(C):
                        mm = pe.transpose(ps_x[:, c * P:(c + 1) * P], xn[:, p0, c * P:(c + 1) * P], ident[:])
                    mm.then_inc(xt_mm, 1)
                if live(w3, N):
                    wait(pe, ol_done, w3 + 1)
                    wait(pe, gated_done, w3)
                    if live(w3 + 2, N):
                        wait(pe, qkv_out, 3 * (w3 + 2) + 2)
                    for c in range(C):
                        mm = triple(pe, ps_mm[:, 1, :], (oh[:, c, :], ol[:, c, :]), [x_[:, c, :] for x_ in wout], c == 0, c == C - 1)
                    mm.then_inc(out_mm, 1)
                if live(w2, N):
                    wait(pe, prt_out, 2 * w2 + 2)
                    wait(pe, qkv_out, 3 * w2 + 3)
                    for h in range(H):
                        mm = pe.matmul(ps_s[:, 0, h * DH:(h + 1) * DH], prt[:, h, :], v[:, p2, h * DH:(h + 1) * DH],
                                       start=True, stop=True)
                    mm.then_inc(pv_mm, 1)

            pipeline(pe, STEPS, HEAD, TAIL, step)


def feed_forward(nc, dram, x1, x2, mods, ident, cols, T):
    NB = T // D
    BPB = NB // 2
    F = 4 * D
    J = F // P
    K = 4
    with ExitStack() as stack:
        m = Memory(nc, stack, "ff")
        w1 = [m.sb(f"w1{n}", [P, C, F], F32R) for n in range(2)]
        w2 = [m.sb(f"w2{n}", [P, J, D], F32R) for n in range(2)]
        stage_stack = ExitStack()
        src1 = dram["w_ff1"].rearrange("(c p) n -> p c n", p=P)
        src2 = dram["w_ff2"].rearrange("(j p) n -> p j n", p=P)
        s = m.sem
        ms = Memory(nc, stage_stack, "ffs")
        weights = Weights(ms, [(src1[:, :, n * D:(n + 1) * D], *(w[:, :, n * D:(n + 1) * D] for w in w1)) for n in range(4)]
                          + [(src2[:, 4 * n:4 * n + 4, :], *(w[:, 4 * n:4 * n + 4, :] for w in w2)) for n in range(4)])
        with nc.Block() as block:
            block.sync(weights.load)
            block.scalar(weights.round_hi)

            @block.vector
            def _(dve):
                weights.rest_lo(dve)
                weights.wait_split(dve)
        stage_stack.close()

        gate = m.sb("gate", [P, 2, D])
        gbias = m.sb("gbias", [P, 2, D])
        xw = m.sb("xw", [P, 2, D])
        sq = m.sb("sq", [P, D])
        ss = m.sb("ss", [P, 2])
        var = m.sb("var", [P, 2])
        half = m.sb("half", [P, 1])
        eps = m.sb("eps", [P, 1])
        rstd = m.sb("rstd", [P, 2])
        xn = m.sb("xn", [P, 2, D])
        hf = m.sb("hf", [P, 2, C, P])
        hh = m.sb("hh", [P, 2, C, K * P], F32R)
        hl = m.sb("hl", [P, 2, C, K * P], F32R)
        g = m.sb("g", [P, 2, D])
        gh = m.sb("gh", [P, 2, D], F32R)
        gl = m.sb("gl", [P, 2, D], F32R)
        xres = m.sb("xres", [P, 2, D])
        xo = m.sb("xo", [P, K, D])
        ps_x = m.ps("ps_x", [P, 2, D])
        ps_f = m.ps("ps_f", [P, 2, D])
        ps_y = m.ps("ps_y", [P, K, D])
        const_loaded, pow_set = s("const_loaded"), s("pow_set")
        x_loaded, xres_loaded, stored = ([s(f"{n}{i}") for i in range(2)] for n in ("x_loaded", "xres_loaded", "stored"))
        sq_done, var_done, rstd_done, xn_done = s("sq_done"), s("var_done"), s("rstd_done"), s("xn_done")
        xt_mm, affine_done, hh_done, hl_done = s("xt_mm"), s("affine_done"), s("hh_done"), s("hl_done")
        f1_mm, gelu_done, gh_done, gl_done, f2_mm = s("f1_mm"), s("gelu_done"), s("gh_done"), s("gl_done"), s("f2_mm")
        gated_done, xres_done, x2_done = s("gated_done"), s("xres_done"), s("x2_done")
        block = stack.enter_context(nc.Block())

        STEPS, HEAD, TAIL = NB + 1, 2, 1
        TURN = {3 * k + 3: k for k in range(K)}

        @block.sync
        def _(sp):
            for b in range(2):
                sp.dma_start(gate[:, b], mods[b, GATE1].partition_broadcast(P)).then_inc(const_loaded, 16)
                sp.dma_start(gbias[:, b], mods[b, GBIAS1].partition_broadcast(P)).then_inc(const_loaded, 16)

            def step(j, u):
                b0, _, _ = back(j, u, 0)
                b1, _, _ = back(j, u, 1)

                def load_res(k):
                    wait(sp, x2_done, K * b1 + k - 1)
                    sp.dma_start(xres[:, k % 2], x1[ds((b1 * K + k) * P, P), :]).then_inc(xres_loaded[k % 2], 16)

                def store(k):
                    wait(sp, x2_done, K * b1 + k + 1)
                    sp.dma_start(x2[ds((b1 * K + k) * P, P), :], xo[:, k]).then_inc(stored[k % 2], 16)

                for k in range(K):
                    if live(b0, NB):
                        wait(sp, xn_done, K * b0 + k - 1)
                        sp.dma_start(xw[:, k % 2], x1[ds((b0 * K + k) * P, P), :]).then_inc(x_loaded[k % 2], 16)
                    if k == 1 and live(b1, NB):
                        load_res(0)
                        load_res(1)
                if live(b1, NB):
                    store(0)
                    load_res(2)
                    store(1)
                    load_res(3)
                    store(2)
                    store(3)

            pipeline(sp, STEPS, HEAD, TAIL, step)
            for p in range(2):
                sp.wait_ge(stored[p], 16 * (K // 2) * NB)

        @block.gpsimd
        def _(pool):
            pool.memset(half[:], -0.5).then_inc(pow_set, 1)
            pool.memset(eps[:], EPS).then_inc(pow_set, 1)
            pool.wait_ge(pow_set, 2)
            pool.wait_ge(const_loaded, 64)

            def step(j, u):
                b0, _, _ = back(j, u, 0)
                b1, _, _ = back(j, u, 1)
                for k in range(K):
                    p = k % 2
                    if live(b0, NB):
                        wait(pool, sq_done, K * b0 + k + 1)
                        pool.tensor_tensor(var[:, p:p + 1], ss[:, p:p + 1], eps[:], ALU.add).then_inc(var_done, 1)
                        wait(pool, var_done, K * b0 + k + 1)
                        pool.tensor_tensor(rstd[:, p:p + 1], var[:, p:p + 1], half[:], ALU.pow).then_inc(rstd_done, 1)
                for k in range(K):
                    p = k % 2
                    if live(b1, NB):
                        wait(pool, xres_loaded[p], 16 * (2 * b1 + k // 2 + 1))
                        pool.tensor_tensor(xres[:, p], xres[:, p], gbias[:, ds(b1 // BPB, 1), :].rearrange("p a d -> p (a d)"),
                                           ALU.add).then_inc(xres_done, 1)
                        wait(pool, xres_done, K * b1 + k + 1)
                        wait(pool, gated_done, K * b1 + k + 1)
                        pool.tensor_tensor(xo[:, k], xo[:, k], xres[:, p], ALU.add).then_inc(x2_done, 1)

            pipeline(pool, STEPS, HEAD, TAIL, step)

        @block.scalar
        def _(act):
            def step(j, u):
                b0, _, _ = back(j, u, 0)
                b1, _, _ = back(j, u, 1)
                for c_ in range(J):
                    if live(b1, NB):
                        wait(act, f1_mm, J * b1 + c_ + 1)
                        wait(act, gl_done, J * b1 + c_ - 1)
                        act.activation(g[:, c_ % 2], ps_f[:, c_ % 2, :], ACT.Gelu_apprx_tanh,
                                       bias=cols[:, 48 + c_:49 + c_]).then_inc(gelu_done, 1)
                    if live(b0, NB) and c_ % 3 == 1 and c_ // 3 < K:
                        k = c_ // 3
                        wait(act, x_loaded[k % 2], 16 * (2 * b0 + k // 2 + 1))
                        act.activation(sq[:], xw[:, k % 2], ACT.Square, scale=D ** -0.5, accum_out=ss[:, k % 2:k % 2 + 1]).then_inc(sq_done, 1)
                    if live(b0, NB) and c_ in TURN:
                        k = TURN[c_]
                        wait(act, xt_mm, K * b0 + k + 1)
                        wait(act, hl_done, K * b0 + k - 1)
                        for c in range(C):
                            a = act.activation(hf[:, k % 2, c], ps_x[:, k % 2, c * P:(c + 1) * P], ACT.Identity,
                                               scale=column(cols, SCALE1, b0 // BPB, c), bias=column(cols, SHIFT1, b0 // BPB, c))
                        a.then_inc(affine_done, 1)

            pipeline(act, STEPS, HEAD, TAIL, step)

        @block.vector
        def _(dve):
            dve.wait_ge(const_loaded, 64)

            def step(j, u):
                b0, q0, _ = back(j, u, 0)
                b1, _, _ = back(j, u, 1)
                for c_ in range(J):
                    p = c_ % 2
                    if live(b0, NB) and c_ % 3 == 2 and c_ // 3 < K:
                        k = c_ // 3
                        wait(dve, rstd_done, K * b0 + k + 1)
                        wait(dve, xt_mm, K * b0 + k - 1)
                        dve.tensor_scalar(xn[:, k % 2], xw[:, k % 2], rstd[:, k % 2:k % 2 + 1], None, ALU.mult).then_inc(xn_done, 1)
                    if live(b1, NB):
                        wait(dve, gelu_done, J * b1 + c_ + 1)
                        wait(dve, f2_mm, J * b1 + c_ - 1)
                        dve.tensor_copy(gh[:, p], g[:, p]).then_inc(gh_done, 1)
                        wait(dve, gh_done, J * b1 + c_ + 1)
                        dve.tensor_tensor(gl[:, p], g[:, p], gh[:, p].bitcast(F32), ALU.subtract).then_inc(gl_done, 1)
                    if live(b0, NB) and c_ in TURN:
                        k = TURN[c_]
                        at = slice(k * P, (k + 1) * P)
                        wait(dve, affine_done, K * b0 + k + 1)
                        wait(dve, f1_mm, J * (b0 - 1))
                        dve.tensor_copy(hh[:, q0, :, at], hf[:, k % 2]).then_inc(hh_done, 1)
                        wait(dve, hh_done, K * b0 + k + 1)
                        dve.tensor_tensor(hl[:, q0, :, at], hf[:, k % 2], hh[:, q0, :, at].bitcast(F32),
                                          ALU.subtract).then_inc(hl_done, 1)
                if live(b1, NB):
                    wait(dve, f2_mm, J * b1 + J)
                    for k in range(K):
                        wait(dve, stored[k % 2], 16 * (2 * (b1 - 1) + k // 2 + 1))
                        dve.tensor_tensor(xo[:, k], ps_y[:, k, :], gate[:, ds(b1 // BPB, 1), :].rearrange("p a d -> p (a d)"),
                                          ALU.mult).then_inc(gated_done, 1)

            pipeline(dve, STEPS, HEAD, TAIL, step)

        @block.tensor
        def _(pe):
            def step(j, u):
                b0, _, _ = back(j, u, 0)
                b1, q1, _ = back(j, u, 1)
                for c_ in range(J + 1):
                    if c_ < J and live(b1, NB):
                        if c_ == 0:
                            wait(pe, hl_done, K * b1 + K)
                        wait(pe, gelu_done, J * b1 + c_ - 1)
                        for c in range(C):
                            mm = triple(pe, ps_f[:, c_ % 2, :], [w[:, c, c_ * P:(c_ + 1) * P] for w in w1],
                                        (hh[:, q1, c, :], hl[:, q1, c, :]), c == 0, c == C - 1)
                        mm.then_inc(f1_mm, 1)
                    if live(b0, NB) and c_ in TURN:
                        k = TURN[c_]
                        wait(pe, xn_done, K * b0 + k + 1)
                        wait(pe, affine_done, K * b0 + k - 1)
                        for c in range(C):
                            mm = pe.transpose(ps_x[:, k % 2, c * P:(c + 1) * P], xn[:, k % 2, c * P:(c + 1) * P], ident[:])
                        mm.then_inc(xt_mm, 1)
                    if c_ > 0 and live(b1, NB):
                        f = c_ - 1
                        wait(pe, gl_done, J * b1 + f + 1)
                        for k in range(K):
                            if f == 0:
                                wait(pe, gated_done, K * (b1 - 1) + k + 1)
                            mm = triple(pe, ps_y[:, k, :], (gh[:, f % 2, k * P:(k + 1) * P], gl[:, f % 2, k * P:(k + 1) * P]),
                                        [w[:, f, :] for w in w2], f == 0, f == J - 1)
                        mm.then_inc(f2_mm, 1)

            pipeline(pe, STEPS, HEAD, TAIL, step)


def project_qkv(nc, dram, x2, q_hl, k_hl, v_d, ident, cols, T):
    NB = T // D
    BPB = NB // 2
    K = 4
    G = 2 * C
    with ExitStack() as stack:
        m = Memory(nc, stack, "qkv")
        w = [m.sb(f"w{n}", [P, C, 3 * D], F32R) for n in range(2)]
        src = dram["w_qkv1"].rearrange("(c p) n -> p c n", p=P)
        weights = Weights(m, [(src[:, :, n * D:(n + 1) * D], *(x_[:, :, n * D:(n + 1) * D] for x_ in w)) for n in range(3)])
        bv = m.sb("bv", [P, D])
        xw = m.sb("xw", [P, 2, D])
        st = m.sb("st", [P, 2, 6])
        mv = m.sb("mv", [P, 2, 2])
        var = m.sb("var", [P, 2])
        half = m.sb("half", [P, 1])
        eps = m.sb("eps", [P, 1])
        rstd = m.sb("rstd", [P, 2])
        xn = m.sb("xn", [P, 2, D])
        hf = m.sb("hf", [P, 2, C, P])
        hh = m.sb("hh", [P, 2, C, K * P], F32R)
        hl = m.sb("hl", [P, 2, C, K * P], F32R)
        f = m.sb("f", [P, 2, D])
        fh = m.sb("fh", [P, 2, D], F32R)
        fl = m.sb("fl", [P, 2, D], F32R)
        vo = m.sb("vo", [P, 2, D])
        ps_x = m.ps("ps_x", [P, 2, D])
        ps_p = m.ps("ps_p", [P, 4, D])
        s = m.sem
        const_loaded, pow_set = s("const_loaded"), s("pow_set")
        x_loaded, f_stored, v_stored = ([s(f"{n}{i}") for i in range(2)] for n in ("x_loaded", "f_stored", "v_stored"))
        stat_done, mv_done, var_done, rstd_done, xn_done = (s(n) for n in ("stat_done", "mv_done", "var_done", "rstd_done", "xn_done"))
        xt_mm, affine_done, hh_done, hl_done = s("xt_mm"), s("affine_done"), s("hh_done"), s("hl_done")
        p_mm, f_done, fh_done, fl_done, v_done = s("p_mm"), s("f_done"), s("fh_done"), s("fl_done"), s("v_done")
        block = stack.enter_context(nc.Block())

        STEPS, HEAD, TAIL = NB + 1, 2, 1
        M = G + K
        TURN = {2 + 2 * k: k for k in range(K)}

        @block.sync
        def _(sp):
            weights.load(sp)
            sp.dma_start(bv[:], dram["b_v1"].partition_broadcast(P)).then_inc(const_loaded, 16)

            def step(j, u):
                b0, _, _ = back(j, u, 0)
                b1, _, _ = back(j, u, 1)

                def load(k):
                    wait(sp, xn_done, K * b0 + k - 1)
                    sp.dma_start(xw[:, k % 2], x2[ds((b0 * K + k) * P, P), :]).then_inc(x_loaded[k % 2], 16)

                for k in range(2):
                    if live(b0, NB):
                        load(k)
                for n in range(M):
                    if live(b1, NB):
                        if n < G:
                            to, c = (q_hl, n) if n < C else (k_hl, n - C)
                            wait(sp, fl_done, G * b1 + n + 1)
                            sp.dma_start(to[0, ds(b1 // BPB * D + c * P, P), ds(b1 % BPB * D, D)], fh[:, n % 2].bitcast(F32)).then_inc(f_stored[n % 2], 16)
                            sp.dma_start(to[1, ds(b1 // BPB * D + c * P, P), ds(b1 % BPB * D, D)], fl[:, n % 2].bitcast(F32)).then_inc(f_stored[n % 2], 16)
                        else:
                            k = n - G
                            wait(sp, v_done, K * b1 + k + 1)
                            sp.dma_start(v_d[ds(b1 // BPB * D, D), ds(b1 % BPB * D + k * P, P)].rearrange("(g t) f -> t g f", t=P),
                                         vo[:, k % 2].rearrange("t (g f) -> t g f", g=C)).then_inc(v_stored[k % 2], 16)
                    if live(b0, NB) and n in (1, 3):
                        load(2 if n == 1 else 3)

            pipeline(sp, STEPS, HEAD, TAIL, step)
            for p in range(2):
                sp.wait_ge(f_stored[p], 32 * (G // 2) * NB)
                sp.wait_ge(v_stored[p], 16 * (K // 2) * NB)

        @block.gpsimd
        def _(pool):
            pool.memset(half[:], -0.5).then_inc(pow_set, 1)
            pool.memset(eps[:], EPS).then_inc(pow_set, 1)
            pool.wait_ge(pow_set, 2)

            def step(j, u):
                b0, _, _ = back(j, u, 0)
                for k in range(K):
                    p = k % 2
                    if live(b0, NB):
                        wait(pool, mv_done, K * b0 + k + 1)
                        pool.tensor_tensor(var[:, p:p + 1], mv[:, p, 1:2], eps[:], ALU.add).then_inc(var_done, 1)
                        wait(pool, var_done, K * b0 + k + 1)
                        pool.tensor_tensor(rstd[:, p:p + 1], var[:, p:p + 1], half[:], ALU.pow).then_inc(rstd_done, 1)

            pipeline(pool, STEPS, HEAD, TAIL, step)

        @block.scalar
        def _(act):
            weights.round_hi(act)

            def step(j, u):
                b0, _, _ = back(j, u, 0)
                b1, _, _ = back(j, u, 1)
                for n in range(M):
                    if live(b1, NB) and n < G:
                        wait(act, p_mm, M * b1 + n + 1)
                        wait(act, fl_done, G * b1 + n - 1)
                        act.activation(f[:, n % 2], ps_p[:, n % 4, :], ACT.Identity, bias=cols[:, 64 + n:65 + n]).then_inc(f_done, 1)
                    if live(b0, NB) and n in TURN:
                        k = TURN[n]
                        wait(act, xt_mm, K * b0 + k + 1)
                        wait(act, hl_done, K * b0 + k - 1)
                        for c in range(C):
                            a = act.activation(hf[:, k % 2, c], ps_x[:, k % 2, c * P:(c + 1) * P], ACT.Identity,
                                               scale=column(cols, SCALE2, b0 // BPB, c), bias=column(cols, SHIFT2, b0 // BPB, c))
                        a.then_inc(affine_done, 1)

            pipeline(act, STEPS, HEAD, TAIL, step)

        @block.vector
        def _(dve):
            weights.rest_lo(dve)
            dve.wait_ge(const_loaded, 16)

            def step(j, u):
                b0, q0, _ = back(j, u, 0)
                b1, _, _ = back(j, u, 1)

                def stats(k):
                    p = k % 2
                    wait(dve, x_loaded[p], 16 * (2 * b0 + k // 2 + 1))
                    dve.bn_stats(st[:, p], xw[:, p]).then_inc(stat_done, 1)
                    wait(dve, stat_done, K * b0 + k + 1)
                    wait(dve, rstd_done, K * b0 + k - 1)

                def aggregate(k):
                    p = k % 2
                    dve.bn_aggr(mv[:, p], st[:, p]).then_inc(mv_done, 1)

                def normalise(k):
                    p = k % 2
                    wait(dve, mv_done, K * b0 + k + 1)
                    wait(dve, rstd_done, K * b0 + k + 1)
                    wait(dve, xt_mm, K * b0 + k - 1)
                    dve.tensor_scalar(xn[:, p], xw[:, p], mv[:, p, 0:1], rstd[:, p:p + 1], ALU.subtract, ALU.mult).then_inc(xn_done, 1)

                for n in range(M):
                    if live(b0, NB) and n % 2 == 0 and n // 2 < K:
                        stats(n // 2)
                    if live(b0, NB) and n % 2 == 1 and n // 2 < K:
                        normalise(n // 2)
                    if live(b1, NB) and n < G:
                        p = n % 2
                        wait(dve, f_done, G * b1 + n + 1)
                        wait(dve, f_stored[p], 32 * ((G // 2) * b1 + n // 2))
                        dve.tensor_copy(fh[:, p], f[:, p]).then_inc(fh_done, 1)
                        wait(dve, fh_done, G * b1 + n + 1)
                        dve.tensor_tensor(fl[:, p], f[:, p], fh[:, p].bitcast(F32), ALU.subtract).then_inc(fl_done, 1)
                    if live(b1, NB) and n >= G:
                        k = n - G
                        wait(dve, p_mm, M * b1 + n + 1)
                        wait(dve, v_stored[k % 2], 16 * (2 * b1 + k // 2))
                        dve.tensor_tensor(vo[:, k % 2], ps_p[:, n % 4, :], bv[:], ALU.add).then_inc(v_done, 1)
                    if live(b0, NB) and n % 2 == 0 and n // 2 < K:
                        aggregate(n // 2)
                    if live(b0, NB) and n in TURN:
                        k = TURN[n]
                        at = slice(k * P, (k + 1) * P)
                        wait(dve, affine_done, K * b0 + k + 1)
                        wait(dve, p_mm, M * (b0 - 1))
                        dve.tensor_copy(hh[:, q0, :, at], hf[:, k % 2]).then_inc(hh_done, 1)
                        wait(dve, hh_done, K * b0 + k + 1)
                        dve.tensor_tensor(hl[:, q0, :, at], hf[:, k % 2], hh[:, q0, :, at].bitcast(F32),
                                          ALU.subtract).then_inc(hl_done, 1)

            pipeline(dve, STEPS, HEAD, TAIL, step)

        @block.tensor
        def _(pe):
            weights.wait_split(pe)

            def step(j, u):
                b0, _, _ = back(j, u, 0)
                b1, q1, _ = back(j, u, 1)
                for n in range(M):
                    if live(b1, NB):
                        if n == 0:
                            wait(pe, hl_done, K * b1 + K)
                        if n < 4:
                            wait(pe, v_done, K * (b1 - 1) + n + 1)
                        else:
                            wait(pe, f_done, G * b1 + n - 3)
                        for c in range(C):
                            if n < G:
                                mm = triple(pe, ps_p[:, n % 4, :], [x_[:, c, n * P:(n + 1) * P] for x_ in w],
                                            (hh[:, q1, c, :], hl[:, q1, c, :]), c == 0, c == C - 1)
                            else:
                                at = slice((n - G) * P, (n - G + 1) * P)
                                mm = triple(pe, ps_p[:, n % 4, :], (hh[:, q1, c, at], hl[:, q1, c, at]),
                                            [x_[:, c, 2 * D:3 * D] for x_ in w], c == 0, c == C - 1)
                        mm.then_inc(p_mm, 1)
                    if live(b0, NB) and n in TURN:
                        k = TURN[n]
                        wait(pe, xn_done, K * b0 + k + 1)
                        wait(pe, affine_done, K * b0 + k - 1)
                        for c in range(C):
                            mm = pe.transpose(ps_x[:, k % 2, c * P:(c + 1) * P], xn[:, k % 2, c * P:(c + 1) * P], ident[:])
                        mm.then_inc(xt_mm, 1)

            pipeline(pe, STEPS, HEAD, TAIL, step)


def full_attention(nc, ident_src, q_hl, k_hl, v_d, o_t, T):
    HG, HD = 4, 32
    S = T // 2
    KT = S // P
    QB = S // D
    ITEMS = 2 * C * QB
    U = KT * HG
    RING = 4
    BANKS = 3
    EARLY = {14: 4, 15: 4}
    AHEAD = [5, 5, 3, 2, 3, 5, 4, 4, 6, 4, 5, 6, 4, 0, 0, 0]
    SPLIT = 4
    TURN = 13
    first_block = sum(EARLY.values())
    AHEAD_AT = [first_block + sum(AHEAD[:k]) for k in range(KT + 1)]
    EARLY_AT = {k: sum(EARLY[i] for i in EARLY if i < k) for k in EARLY}
    assert AHEAD_AT[KT] == U
    PE_SUMS = (4, 7, 10, 12, 15)
    POOL_SUMS = [k for k in range(KT) if k not in PE_SUMS]
    POOL_OPS = len(POOL_SUMS) - 1
    pool_after = {k: max(n, 1) for n, k in enumerate(POOL_SUMS)}
    LOOP = 8

    def count(item, per_item, done):
        return per_item * item + (done + per_item)

    with ExitStack() as stack:
        m = Memory(nc, stack, "att")
        kst = [m.sb(f"kst{n}", [98, HG, S], F32R) for n in range(2)]
        qst = [m.sb(f"qst{n}", [98, HG, D], F32R) for n in range(4)]
        vt = [m.sb(f"vt{n}", [P, KT, HG * HD]) for n in range(2)]
        prob = m.sb("prob", [P, RING, HG, D])
        acc = m.sb("acc", [P, 2, HG, D])
        scale = m.sb("scale", [P, HD])
        mx = m.sb("mx", [P, U])
        m16 = m.sb("m16", [P, 16])
        ident = m.sb("ident", [P, P])
        nmh = m.sb("nmh", [16, 2, P], F32R)
        nml = m.sb("nml", [16, 2, P], F32R)
        oraw = m.sb("oraw", [P, D])
        rec = m.sb("rec", [P, D])
        on = m.sb("on", [P, D])
        ps_st = m.ps("ps_st", [P, BANKS, D])
        ps_mx = m.ps("ps_mx", [P, BANKS, D])
        ps_o = m.ps("ps_o", [P, D])
        ps_sum = m.ps("ps_sum", [P, D])
        s = m.sem
        const_done, ident_loaded, o_stored = s("const_done"), s("ident_loaded"), s("o_stored")
        q_loaded = [s(f"q_loaded{n}") for n in range(4)]
        k_loaded, v_loaded, negmax_loaded = ([s(f"{x}{n}") for n in range(2)] for x in ("k_loaded", "v_loaded", "negmax_loaded"))
        ahead_mm, max_done, allmax_done, allmax_mm, negmax_done = (s(n) for n in (
            "ahead_mm", "max_done", "allmax_done", "allmax_mm", "negmax_done"))
        half_max = s("half_max")
        score_mm, exp_done, pv_mm, pool_done, sum_mm, rec_done, oraw_done, on_done = (s(n) for n in (
            "score_mm", "exp_done", "pv_mm", "pool_done", "sum_mm", "rec_done", "oraw_done", "on_done"))
        block = stack.enter_context(nc.Block())

        def drive(eng, ahead, tile, flush):
            ahead()
            for kt in range(SPLIT):
                tile(0, 0, kt)
            with eng.Fori(0, ITEMS // LOOP - 1) as j:
                for r in range(LOOP):
                    for kt in range(SPLIT, KT):
                        tile(j, r, kt)
                    for kt in range(SPLIT):
                        tile(j, r + 1, kt)
            j = ITEMS // LOOP - 1
            for r in range(LOOP):
                for kt in range(SPLIT, KT):
                    tile(j, r, kt)
                if r + 1 < LOOP:
                    for kt in range(SPLIT):
                        tile(j, r + 1, kt)
            flush()

        @block.sync
        def _(sp):
            def load_q(j, r):
                n = 2 * j + r // QB
                for row, part in ((0, 0), (1, 1), (2, 0)):
                    sp.dma_start(qst[r % 4][HD * row:HD * row + HD].bitcast(F32),
                                 q_hl[part, ds(n * P, P), r % QB * D:(r % QB + 1) * D].rearrange(
                                     "(h d) t -> d h t", d=HD)).then_inc(q_loaded[r % 4], 16)

            def load_kv(j, r):
                n = 2 * j + r // QB
                p = (r // QB) % 2
                for row, part in ((0, 0), (1, 0), (2, 1)):
                    sp.dma_start(kst[p][HD * row:HD * row + HD].bitcast(F32),
                                 k_hl[part, ds(n * P, P), :].rearrange(
                                     "(h d) t -> d h t", d=HD)).then_inc(k_loaded[p], 16)
                sp.dma_start(vt[p][:].rearrange("p k f -> p (k f)"), v_d[ds(n * P, P), :]).then_inc(v_loaded[p], 16)

            def load_negmax(j, r):
                wait(sp, negmax_done, count(LOOP * j + r, 1, 1))
                for row, t in ((96, nmh), (97, nml)):
                    sp.dma_start(qst[r % 4][row:row + 1].bitcast(F32).rearrange("o h (t q) -> o (h t) q", q=P),
                                 t[:, r % 2, :].bitcast(F32)).then_inc(negmax_loaded[r % 2], 16)

            def store(j, r):
                item = LOOP * j + r
                n = 2 * j + r // QB
                wait(sp, on_done, count(item, 1, 1))
                sp.dma_start(o_t[ds(n * P, P), r % QB * D:(r % QB + 1) * D], on[:]).then_inc(o_stored, 16)

            def ahead():
                sp.dma_start(ident[:], ident_src).then_inc(ident_loaded, 16)
                load_q(0, 0)
                load_kv(0, 0)
                load_q(0, 1)
                load_negmax(0, 0)

            def tile(j, r, kt):
                item = LOOP * j + r
                if kt == 3 and not (isinstance(item, int) and item == 0):
                    store(j, r - 1)
                if kt == 4:
                    wait(sp, score_mm, count(item, U, 0))
                    wait(sp, pv_mm, count(item, KT, 0))
                    if r % QB == 0 and live(item + QB, ITEMS):
                        load_kv(j, r + QB)
                    if live(item + 2, ITEMS):
                        load_q(j, r + 2)
                if kt == TURN and live(item + 1, ITEMS):
                    load_negmax(j, r + 1)

            def flush():
                store(ITEMS // LOOP - 1, LOOP - 1)
                sp.wait_ge(o_stored, 16 * ITEMS)

            drive(sp, ahead, tile, flush)

        @block.gpsimd
        def _(pool):
            pool.sem_inc(pool_done, POOL_OPS)
            pool.memset(scale[:], float(D) ** 0.5).then_inc(const_done, 1)
            for n in range(2):
                pool.wait_ge(const_done, n + 1)
                pool.memset(kst[n][96:98].bitcast(F32), 1.0).then_inc(const_done, 1)

            def tile(j, r, kt):
                item = LOOP * j + r
                if kt in POOL_SUMS and kt != POOL_SUMS[0]:
                    wait(pool, exp_done, count(item, U, HG * (kt + 1)))
                    a = acc[:, r % 2]
                    if kt == POOL_SUMS[1]:
                        wait(pool, sum_mm, count(item - 2, 1, 1))
                        first = prob[:, POOL_SUMS[0] % RING]
                    else:
                        wait(pool, pool_done, count(item, POOL_OPS, pool_after[kt] - 1))
                        first = a
                    pool.tensor_tensor(a, first, prob[:, kt % RING], ALU.add).then_inc(pool_done, 1)

            drive(pool, lambda: None, tile, lambda: None)

        @block.scalar
        def _(act):
            act.sem_inc(exp_done, U)
            act.sem_inc(oraw_done, 1)

            def copy_out(j, r):
                item = LOOP * j + r
                wait(act, pv_mm, count(item, KT, KT))
                wait(act, on_done, count(item - 1, 1, 1))
                act.activation(oraw[:], ps_o[:], ACT.Copy).then_inc(oraw_done, 1)

            def tile(j, r, kt):
                item = LOOP * j + r
                for h in range(HG):
                    wait(act, score_mm, count(item, U, HG * kt + h + 1))
                    if h == 0:
                        wait(act, pv_mm, count(item, KT, kt - RING + 1))
                        old = (kt - RING) % KT
                        if old in POOL_SUMS:
                            of = item if kt >= RING else item - 1
                            wait(act, pool_done, count(of, POOL_OPS, pool_after[old]))
                    act.activation(prob[:, kt % RING, h], ps_st[:, (HG * kt + h) % BANKS, :], ACT.Exp).then_inc(exp_done, 1)
                    if kt == 0 and h == 3 and not (isinstance(item, int) and item == 0):
                        copy_out(j, r - 1)

            drive(act, lambda: None, tile, lambda: copy_out(ITEMS // LOOP - 1, LOOP - 1))

        @block.vector
        def _(dve):
            for sem, n in ((max_done, U), (allmax_done, 1), (negmax_done, 1), (rec_done, 2), (on_done, 1)):
                dve.sem_inc(sem, n)

            def reduce_blocks(j, r, a, b):
                item = LOOP * j + r
                for n in range(a, b):
                    wait(dve, ahead_mm, count(item, U, n + 1))
                    if n == 0:
                        wait(dve, allmax_done, count(item, 1, 0))
                    dve.tensor_reduce(mx[:, n:n + 1], ps_mx[:, n % BANKS, :], AX.X, ALU.max).then_inc(max_done, 1)
                    if n == U - 1:
                        wait(dve, max_done, count(item, U, U))
                        wait(dve, allmax_mm, item)
                        dve.tensor_reduce(m16[:], mx[:].rearrange("p (b k) -> p b k", b=16), AX.X, ALU.max,
                                          negate=True).then_inc(allmax_done, 1)

            def split_max(j, r):
                item = LOOP * j + r
                wait(dve, allmax_mm, item + 1)
                wait(dve, negmax_loaded[r % 2], 32 * (4 * j + r // 2))
                dve.tensor_copy(nmh[:, r % 2], ps_mx[0:16, 1, 0:P]).then_inc(half_max, 1)
                wait(dve, half_max, item + 1)
                dve.tensor_tensor(nml[:, r % 2], ps_mx[0:16, 1, 0:P], nmh[:, r % 2].bitcast(F32), ALU.subtract).then_inc(negmax_done, 1)

            def finish(j, r, part):
                item = LOOP * j + r
                at = slice(part * D // 2, (part + 1) * D // 2)
                if part == 0:
                    wait(dve, sum_mm, count(item, 1, 1))
                    wait(dve, on_done, count(item, 1, 0))
                dve.reciprocal(rec[:, at], ps_sum[:, at]).then_inc(rec_done, 1)
                if part == 1:
                    wait(dve, rec_done, count(item, 2, 2))
                    wait(dve, oraw_done, count(item, 1, 1))
                    wait(dve, o_stored, 16 * item)
                    dve.tensor_tensor(on[:], oraw[:], rec[:], ALU.mult).then_inc(on_done, 1)

            def ahead():
                reduce_blocks(0, 0, 0, U)
                split_max(0, 0)
                reduce_blocks(0, 1, 0, first_block)

            def tile(j, r, kt):
                item = LOOP * j + r
                if live(item + 1, ITEMS):
                    reduce_blocks(j, r + 1, AHEAD_AT[kt], AHEAD_AT[kt + 1])
                    if kt == TURN:
                        split_max(j, r + 1)
                if kt in EARLY and live(item + 2, ITEMS):
                    reduce_blocks(j, r + 2, EARLY_AT[kt], EARLY_AT[kt] + EARLY[kt])
                if kt in (2, 3) and not (isinstance(item, int) and item == 0):
                    finish(j, r - 1, kt - 2)

            def flush():
                for part in range(2):
                    finish(ITEMS // LOOP - 1, LOOP - 1, part)

            drive(dve, ahead, tile, flush)

        @block.tensor
        def _(pe):
            for sem, n in ((ahead_mm, U), (score_mm, U), (pv_mm, KT), (sum_mm, 1)):
                pe.sem_inc(sem, n)
            pe.wait_ge(const_done, 3)
            pe.wait_ge(ident_loaded, 16)

            def blocks(j, r, a, b):
                item = LOOP * j + r
                for n in range(a, b):
                    if n == 0:
                        wait(pe, q_loaded[r % 4], 48 * (2 * j + r // 4 + 1))
                        wait(pe, k_loaded[(r // QB) % 2], 48 * (j + r // (2 * QB) + 1))
                        wait(pe, max_done, count(item, U, 0))
                    elif n == 1:
                        wait(pe, negmax_done, count(item, 1, 0))
                    elif n >= BANKS:
                        wait(pe, max_done, count(item, U, n - BANKS + 1))
                    h, t, k = n // 16, (n // 4) % 4, n % 4
                    pe.matmul(ps_mx[:, n % BANKS, :], qst[r % 4][0:96, h, t * P:(t + 1) * P],
                              kst[(r // QB) % 2][0:96, h, k * D:(k + 1) * D], start=True, stop=True).then_inc(ahead_mm, 1)

            def turn_max(j, r):
                item = LOOP * j + r
                wait(pe, allmax_done, count(item, 1, 1))
                pe.transpose(ps_mx[0:16, 1, 0:P], m16[:], ident[:]).then_inc(allmax_mm, 1)

            def score(j, r, kt, h):
                item = LOOP * j + r
                n = HG * kt + h
                if n == 0:
                    wait(pe, negmax_loaded[r % 2], 32 * (4 * j + r // 2 + 1))
                    wait(pe, exp_done, count(item, U, 0))
                elif n >= BANKS:
                    wait(pe, exp_done, count(item, U, n - BANKS + 1))
                pe.matmul(ps_st[:, n % BANKS, :], kst[(r // QB) % 2][:, h, kt * P:(kt + 1) * P], qst[r % 4][:, h, :],
                          start=True, stop=True).then_inc(score_mm, 1)

            def add_sums(rhs, start, stop):
                for h in range(HG):
                    mm = pe.matmul(ps_sum[HD * h:HD * h + HD, :], scale[:], rhs[:, h, :], start=start, stop=stop,
                                   skip_group_check=True)
                return mm

            def sums(j, r, kt):
                item = LOOP * j + r
                wait(pe, exp_done, count(item, U, HG * (kt + 1)))
                if kt == PE_SUMS[0]:
                    wait(pe, rec_done, count(item, 2, 0))
                add_sums(prob[:, kt % RING], kt == PE_SUMS[0], False)

            def values(j, r, kt):
                item = LOOP * j + r
                p = (r // QB) % 2
                wait(pe, exp_done, count(item, U, HG * (kt + 1)))
                if kt == 0:
                    wait(pe, oraw_done, count(item, 1, 0))
                    wait(pe, v_loaded[p], 16 * (j + r // (2 * QB) + 1))
                for h in range(HG):
                    mm = pe.matmul(ps_o[HD * h:HD * h + HD, :], vt[p][:, kt, HD * h:HD * h + HD], prob[:, kt % RING, h, :],
                                   start=kt == 0, stop=kt == KT - 1, skip_group_check=True)
                mm.then_inc(pv_mm, 1)

            def finish(j, r):
                wait(pe, pool_done, count(LOOP * j + r, POOL_OPS, POOL_OPS))
                add_sums(acc[:, r % 2], False, True).then_inc(sum_mm, 1)

            def ahead():
                blocks(0, 0, 0, U)
                turn_max(0, 0)
                blocks(0, 1, 0, first_block)

            def tile(j, r, kt):
                item = LOOP * j + r
                first = isinstance(item, int) and item == 0
                if kt in EARLY:
                    of, a, b = r + 2, EARLY_AT[kt], EARLY_AT[kt] + EARLY[kt]
                else:
                    of, a, b = r + 1, AHEAD_AT[kt], AHEAD_AT[kt + 1]
                if not live(LOOP * j + of, ITEMS):
                    a = b
                old_r, old_kt = (r, kt - 1) if kt > 0 else (r - 1, KT - 1)
                summed = old_kt in PE_SUMS and not (first and kt == 0)
                slots = [0, 4, 1, 5, 3, 2] if summed or kt == 2 else [0, 4, 1, 5, 3, 3]
                cut = [a]
                for slot in range(6):
                    cut.append(cut[-1] + slots[:b - a].count(slot))
                assert cut[-1] == b
                score(j, r, kt, 0)
                blocks(j, of, cut[0], cut[1])
                score(j, r, kt, 1)
                blocks(j, of, cut[1], cut[2])
                if summed:
                    sums(j, old_r, old_kt)
                if kt == 2 and not first:
                    finish(j, r - 1)
                blocks(j, of, cut[2], cut[3])
                if kt > 0 or not first:
                    values(j, old_r, old_kt)
                blocks(j, of, cut[3], cut[4])
                if kt == TURN and live(item + 1, ITEMS):
                    turn_max(j, r + 1)
                score(j, r, kt, 2)
                blocks(j, of, cut[4], cut[5])
                score(j, r, kt, 3)
                blocks(j, of, cut[5], cut[6])

            def flush():
                sums(ITEMS // LOOP - 1, LOOP - 1, KT - 1)
                values(ITEMS // LOOP - 1, LOOP - 1, KT - 1)
                finish(ITEMS // LOOP - 1, LOOP - 1)

            drive(pe, ahead, tile, flush)


def output(nc, dram, o_t, x2, out, mods, T):
    N = T // P
    WPB = N // 2
    with ExitStack() as stack:
        m = Memory(nc, stack, "out")
        w = [m.sb(f"w{n}", [P, C, D], F32R) for n in range(2)]
        weights = Weights(m, [(dram["wp_t"].rearrange("(c p) n -> p c n", p=P), *(x_[:] for x_ in w))])
        bp = m.sb("bp", [P, D])
        scale = m.sb("scale", [P, 2, D])
        shift = m.sb("shift", [P, 2, D])
        ot = m.sb("ot", [P, 2, C, P])
        oh = m.sb("oh", [P, 2, C, P], F32R)
        ol = m.sb("ol", [P, 2, C, P], F32R)
        xres = m.sb("xres", [P, 2, D])
        h1 = m.sb("h1", [P, 2, D])
        hs = m.sb("hs", [P, 2, D])
        st = m.sb("st", [P, 2, 6])
        mv = m.sb("mv", [P, 2, 2])
        var = m.sb("var", [P, 2])
        half = m.sb("half", [P, 1])
        eps = m.sb("eps", [P, 1])
        rstd = m.sb("rstd", [P, 2])
        ln = m.sb("ln", [P, 2, D])
        y = m.sb("y", [P, 2, D])
        ps = m.ps("ps", [P, 2, D])
        s = m.sem
        const_loaded, pow_set = s("const_loaded"), s("pow_set")
        o_loaded, xres_loaded, stored = ([s(f"{x_}{n}") for n in range(2)] for x_ in ("o_loaded", "xres_loaded", "stored"))
        oh_done, ol_done, mm_done, xres_done, h1_done, stat_done, mv_done, var_done, rstd_done, ln_done, scaled_done, hs_done, y_done = (
            s(n) for n in ("oh_done", "ol_done", "mm_done", "xres_done", "h1_done", "stat_done", "mv_done", "var_done",
                           "rstd_done", "ln_done", "scaled_done", "hs_done", "y_done"))
        block = stack.enter_context(nc.Block())
        STEPS, HEAD, TAIL = N + 4, 4, 4

        def of_batch(t, w_):
            return t[:, ds(w_ // WPB, 1), :].rearrange("p a d -> p (a d)")

        @block.sync
        def _(sp):
            weights.load(sp)
            sp.dma_start(bp[:], dram["b_p"].partition_broadcast(P)).then_inc(const_loaded, 16)
            for b in range(2):
                sp.dma_start(scale[:, b], mods[b, SCALE2].partition_broadcast(P)).then_inc(const_loaded, 16)
                sp.dma_start(shift[:, b], mods[b, SHIFT2].partition_broadcast(P)).then_inc(const_loaded, 16)

            def step(j, u):
                w0, p0, _ = back(j, u, 0)
                if live(w0, N):
                    wait(sp, ol_done, w0 - 1)
                    sp.dma_start(ot[:, p0], o_t[ds(w0 // WPB * D, D), ds(w0 % WPB * P, P)].rearrange("(c p) t -> p c t", p=P)).then_inc(o_loaded[p0], 16)
                    wait(sp, h1_done, w0 - 1)
                    sp.dma_start(xres[:, p0], x2[ds(w0 * P, P), :]).then_inc(xres_loaded[p0], 16)
                w4, p4, _ = back(j, u, 4)
                if live(w4, N):
                    wait(sp, y_done, w4 + 1)
                    sp.dma_start(out[ds(w4 * P, P), :], y[:, p4]).then_inc(stored[p4], 16)

            pipeline(sp, STEPS, HEAD, TAIL, step)
            for p in range(2):
                sp.wait_ge(stored[p], 16 * (N // 2))

        @block.gpsimd
        def _(pool):
            pool.memset(half[:], -0.5).then_inc(pow_set, 1)
            pool.memset(eps[:], EPS).then_inc(pow_set, 1)
            pool.wait_ge(pow_set, 2)
            pool.wait_ge(const_loaded, 80)

            def step(j, u):
                w1, p1, k1 = back(j, u, 1)
                w2, p2, _ = back(j, u, 2)
                if live(w2, N):
                    wait(pool, mv_done, w2 + 1)
                    pool.tensor_tensor(var[:, p2:p2 + 1], mv[:, p2, 1:2], eps[:], ALU.add).then_inc(var_done, 1)
                    wait(pool, var_done, w2 + 1)
                    pool.tensor_tensor(rstd[:, p2:p2 + 1], var[:, p2:p2 + 1], half[:], ALU.pow).then_inc(rstd_done, 1)
                if live(w1, N):
                    wait(pool, xres_loaded[p1], 16 * (k1 + 1))
                    pool.tensor_tensor(xres[:, p1], xres[:, p1], bp[:], ALU.add).then_inc(xres_done, 1)
                if live(w2, N):
                    wait(pool, y_done, w2 - 1)
                    pool.tensor_tensor(hs[:, p2], h1[:, p2], of_batch(shift, w2), ALU.add).then_inc(hs_done, 1)

            pipeline(pool, STEPS, HEAD, TAIL, step)

        @block.scalar
        def _(act):
            weights.round_hi(act)

            def step(j, u):
                w1, p1, k1 = back(j, u, 1)
                if live(w1, N):
                    wait(act, o_loaded[p1], 16 * (k1 + 1))
                    wait(act, mm_done, w1 - 1)
                    act.activation(oh[:, p1], ot[:, p1], ACT.Copy).then_inc(oh_done, 1)

            pipeline(act, STEPS, HEAD, TAIL, step)

        @block.vector
        def _(dve):
            weights.rest_lo(dve)
            dve.wait_ge(const_loaded, 80)

            def step(j, u):
                w1, p1, _ = back(j, u, 1)
                w2, p2, _ = back(j, u, 2)
                w3, p3, k3 = back(j, u, 3)
                if live(w1, N):
                    wait(dve, oh_done, w1 + 1)
                    wait(dve, mm_done, w1 - 1)
                    dve.tensor_tensor(ol[:, p1], ot[:, p1], oh[:, p1].bitcast(F32), ALU.subtract).then_inc(ol_done, 1)
                if live(w2, N):
                    wait(dve, mm_done, w2 + 1)
                    wait(dve, xres_done, w2 + 1)
                    wait(dve, hs_done, w2 - 1)
                    dve.tensor_tensor(h1[:, p2], ps[:, p2, :], xres[:, p2], ALU.add).then_inc(h1_done, 1)
                    wait(dve, h1_done, w2 + 1)
                    dve.bn_stats(st[:, p2], h1[:, p2]).then_inc(stat_done, 1)
                    wait(dve, stat_done, w2 + 1)
                if live(w3, N):
                    wait(dve, rstd_done, w3 + 1)
                    dve.tensor_scalar(ln[:, p3], h1[:, p3], mv[:, p3, 0:1], rstd[:, p3:p3 + 1], ALU.subtract, ALU.mult).then_inc(ln_done, 1)
                if live(w2, N):
                    dve.bn_aggr(mv[:, p2], st[:, p2]).then_inc(mv_done, 1)
                if live(w3, N):
                    wait(dve, ln_done, w3 + 1)
                    dve.tensor_tensor(ln[:, p3], ln[:, p3], of_batch(scale, w3), ALU.mult).then_inc(scaled_done, 1)
                    wait(dve, scaled_done, w3 + 1)
                    wait(dve, hs_done, w3 + 1)
                    wait(dve, stored[p3], 16 * k3)
                    dve.tensor_tensor(y[:, p3], ln[:, p3], hs[:, p3], ALU.add).then_inc(y_done, 1)

            pipeline(dve, STEPS, HEAD, TAIL, step)

        @block.tensor
        def _(pe):
            weights.wait_split(pe)

            def step(j, u):
                w1, p1, _ = back(j, u, 1)
                if live(w1, N):
                    wait(pe, ol_done, w1 + 1)
                    wait(pe, h1_done, w1 - 1)
                    for c in range(C):
                        mm = triple(pe, ps[:, p1, :], (oh[:, p1, c], ol[:, p1, c]), [x_[:, c, :] for x_ in w], c == 0, c == C - 1)
                    mm.then_inc(mm_done, 1)

            pipeline(pe, STEPS, HEAD, TAIL, step)


def build(nc, dram, out):
    nc.disable_value_cache = True
    T = out.shape[0]
    x1 = nc.dram_tensor("x1", [T, D], F32, kind="Internal").ap()
    x2 = nc.dram_tensor("x2", [T, D], F32, kind="Internal").ap()
    mods = nc.dram_tensor("mods", [2, MODS, D], F32, kind="Internal").ap()
    q_hl = nc.dram_tensor("q_hl", [2, 2 * D, T // 2], F32, kind="Internal").ap()
    k_hl = nc.dram_tensor("k_hl", [2, 2 * D, T // 2], F32, kind="Internal").ap()
    v_d = nc.dram_tensor("v_d", [2 * D, T // 2], F32, kind="Internal").ap()
    o_t = nc.dram_tensor("o_t", [2 * D, T // 2], F32, kind="Internal").ap()
    with nc.sbuf_tensor("ident", [P, P], F32) as ident, nc.sbuf_tensor("cols", [P, 72], F32) as cols:
        modulation(nc, dram, mods, ident, cols)
        window_attention(nc, dram, dram["x"], x1, mods, ident, cols, T)
        feed_forward(nc, dram, x1, x2, mods, ident, cols, T)
        project_qkv(nc, dram, x2, q_hl, k_hl, v_d, ident, cols, T)
    full_attention(nc, dram["ident"], q_hl, k_hl, v_d, o_t, T)
    output(nc, dram, o_t, x2, out, mods, T)


def kernel(**inputs):
    import numpy as np
    import concourse.bacc as bacc
    from concourse.bass_utils import run_bass_kernel_spmd

    x = np.asarray(inputs["x"])
    B, L, _ = x.shape
    DH = 64
    freqs = (1.0 / 10000.0 ** (np.arange(0, DH, 2, dtype=np.float32) / DH)).astype(np.float32)
    ang = np.arange(P, dtype=np.float32)[:, None] * freqs[None, :]
    sin = np.repeat(np.sin(ang), 2, axis=-1).astype(np.float32)
    cos = np.repeat(np.cos(ang), 2, axis=-1).astype(np.float32)
    sin = np.concatenate([-sin[:, :DH // 2], sin[:, DH // 2:]], axis=-1)
    w1 = np.asarray(inputs["L1_cond_Wqkv"]).reshape(16, 32, 3, D).transpose(3, 2, 0, 1).reshape(D, 3 * D)
    b1 = np.asarray(inputs["L1_cond_bqkv"]).reshape(16, 32, 3).transpose(2, 0, 1).reshape(3, D)
    arrays = {
        "x": x.reshape(B * L, D), "cond": inputs["cond_1024"],
        "w_ada": inputs["L0_cond_W_ada"], "b_ada": inputs["L0_cond_b_ada"],
        "scale1": inputs["L0_cond_scale1"], "scale2": inputs["L0_cond_scale2"],
        "w_qkv0": inputs["L0_cond_W_qkv"], "b_qkv0": inputs["L0_cond_b_qkv"],
        "w_out0": inputs["L0_cond_W_out"], "b_out": inputs["L0_cond_b_out"],
        "w_ff1": inputs["L0_cond_W_ff1"], "b_ff1": inputs["L0_cond_b_ff1"],
        "w_ff2": inputs["L0_cond_W_ff2"], "b_ff2": inputs["L0_cond_b_ff2"],
        "ln_g": inputs["L1_cond_ln_g"], "ln_b": inputs["L1_cond_ln_b"],
        "wg_t": np.asarray(inputs["L1_cond_Wg"]).T, "bg": inputs["L1_cond_bg"],
        "wb_t": np.asarray(inputs["L1_cond_Wb"]).T, "bb": inputs["L1_cond_bb"],
        "w_qkv1": w1, "b_q1": b1[0], "b_k1": b1[1], "b_v1": b1[2],
        "wp_t": np.asarray(inputs["L1_cond_Wp"]).T, "b_p": inputs["L1_cond_bp"],
        "cos": cos, "sin": sin, "ident": np.eye(P, dtype=np.float32),
    }
    arrays = {f"in_{k}": np.ascontiguousarray(v) for k, v in arrays.items()}
    nc = bacc.Bacc("TRN2", target_bir_lowering=False, num_devices=1)
    dram = {k[3:]: nc.dram_tensor(k, list(v.shape), mybir.dt.from_np(v.dtype), kind="ExternalInput").ap()
            for k, v in arrays.items()}
    out = nc.dram_tensor("out", [B * L, D], F32, kind="ExternalOutput").ap()
    build(nc, dram, out)
    r = run_bass_kernel_spmd(nc, [arrays], core_ids=[0])
    return np.asarray(r.results[0]["out"]).reshape(B, L, D)
```

```python
from contextlib import ExitStack

import concourse.bass as bass
from concourse import mybir

F32 = mybir.dt.float32
F32R = mybir.dt.float32r
ALU = mybir.AluOpType
ACT = mybir.ActivationFunctionType
AX = mybir.AxisListType
ds = bass.ds

P = 128
D = 512
C = D // P
EPS = 1e-5

SCALE0, SHIFT0, SCALE1, SHIFT1, SCALE2, SHIFT2, GATE0, GBIAS0, GATE1, GBIAS1 = range(10)
MODS = 10
COLS = 6


def wait(eng, sem, value):
    if not isinstance(value, int) or value > 0:
        eng.wait_ge(sem, value)


def live(index, count):
    return not isinstance(index, int) or 0 <= index < count


def back(j, u, lag):
    t = u - lag
    return 2 * j + t, t % 2, j + t // 2


def pipeline(eng, steps, head, tail, step):
    for s in range(head):
        step(*divmod(s, 2))
    with eng.Fori(head // 2, (steps - tail) // 2) as j:
        for u in range(2):
            step(j, u)
    for s in range(steps - tail, steps):
        step(*divmod(s, 2))


def triple(pe, out, lhs, rhs, start, stop):
    pe.matmul(out, lhs[1], rhs[0], start=start, stop=False)
    pe.matmul(out, lhs[0], rhs[1], start=False, stop=False)
    return pe.matmul(out, lhs[0], rhs[0], start=False, stop=stop)


class Memory:

    def __init__(self, nc, stack, phase):
        self.nc, self.stack, self.phase = nc, stack, phase
        self.sems = []

    def sb(self, name, shape, dt=F32):
        return self.stack.enter_context(self.nc.sbuf_tensor(f"{self.phase}_{name}", shape, dt))

    def hi_lo(self, name, shape):
        hi = self.sb(f"{name}_hi", shape, F32R)
        at = self.nc.sbuf_base
        lo = self.sb(f"{name}_lo", shape, F32R)
        raw = self.nc.alloc_sbuf_tensor_at(f"{self.phase}_{name}_raw", shape, F32, offset=at)
        return [hi, lo], raw

    def ps(self, name, shape, dt=F32):
        return self.stack.enter_context(self.nc.psum_tensor(f"{self.phase}_{name}", shape, dt))

    def sem(self, name):
        self.sems.append(self.stack.enter_context(self.nc.semaphore(f"{self.phase}_{name}")))
        return self.sems[-1]

    def clear(self):
        with self.nc.Block() as block:
            @block.gpsimd
            def _(pool):
                for sem in self.sems:
                    pool.sem_clear(sem)


class Weights:

    def __init__(self, mem, chunks):
        self.chunks = chunks
        self.loaded = [mem.sem(f"w_loaded{n}") for n in range(len(chunks))]
        self.hi_done = mem.sem("w_hi_done")
        self.lo_done = mem.sem("w_lo_done")

    def load(self, eng, start=0, end=None):
        for (source, raw, _, _), loaded in list(zip(self.chunks, self.loaded))[start:end]:
            eng.dma_start(raw, source).then_inc(loaded, 16)

    def round_hi(self, act, start=0, end=None):
        for (_, raw, hi, _), loaded in list(zip(self.chunks, self.loaded))[start:end]:
            act.wait_ge(loaded, 16)
            act.activation(hi, raw, ACT.Copy).then_inc(self.hi_done, 1)

    def rest_lo(self, dve, start=0, end=None):
        for n, (_, raw, hi, lo) in list(enumerate(self.chunks))[start:end]:
            dve.wait_ge(self.hi_done, n + 1)
            dve.tensor_tensor(lo, raw, hi.bitcast(F32), ALU.subtract).then_inc(self.lo_done, 1)

    def wait_split(self, pe, chunks=None):
        pe.wait_ge(self.lo_done, chunks or len(self.chunks))


def modulation(nc, dram, mods, ident, cols, next_weights):
    with ExitStack() as stack:
        m = Memory(nc, stack, "mod")
        B = 2
        VEC = ["scale1", "scale2", "b_out", "b_ff2", "ln_g", "ln_b"]
        cond_rows = m.sb("cond_rows", [B * C, P])
        cond = m.sb("cond", [P, B, C])
        sig = m.sb("sig", [P, B, C])
        silu = m.sb("silu", [P, B, C])
        w_ada = m.sb("w_ada", [P, C, 6 * D])
        w_style = w_ada[:, :, 0:2 * D].rearrange("p c (n d) -> p c n d", n=2)
        bias = m.sb("bias", [B, 8, D])
        vec = m.sb("vec", [B, len(VEC), D])
        raw = bias
        made = vec
        rows = m.sb("rows", [72, P])
        ps = m.ps("ps", [P, 8, D])
        cond_loaded, vec_loaded, style_loaded = (m.sem(x) for x in ("cond_loaded", "vec_loaded", "style_loaded"))
        ada_loaded = [m.sem(f"ada_loaded{n}") for n in range(6)]
        cond_mm, cond_done = m.sem("cond_mm"), m.sem("cond_done")
        exp_done, sig_done, silu_done, raw_mm, raw_done, made_done = (m.sem(x) for x in (
            "exp_done", "sig_done", "silu_done", "raw_mm", "raw_done", "made_done"))
        table_stored, rows_loaded, cols_mm, cols_done = (m.sem(x) for x in (
            "table_stored", "rows_loaded", "cols_mm", "cols_done"))
        inner = stack.enter_context(ExitStack())
        block = inner.enter_context(nc.Block())

        MADE = [SCALE0, SCALE1, GBIAS0, GBIAS1, SCALE2, SHIFT2]
        RAW = {SHIFT0: 0, GATE0: 2, SHIFT1: 3, GATE1: 5}

        @block.sync
        def _(sp):
            sp.dma_start(cond_rows[:], dram["cond"].rearrange("b (c p) -> (b c) p", p=P)).then_inc(cond_loaded, 16)
            sp.dma_start(ident[:], dram["ident"]).then_inc(cond_loaded, 16)
            for n in range(6):
                sp.dma_start(w_ada[:, :, n * D:(n + 1) * D],
                             dram["w_ada"].rearrange("(c p) n -> p c n", p=P)[:, :, n * D:(n + 1) * D]
                             ).then_inc(ada_loaded[n], 16)
            sp.dma_start(bias[:, 0:6, :].rearrange("b n d -> b (n d)"),
                         dram["b_ada"].partition_broadcast(B)).then_inc(vec_loaded, 16)
            sp.dma_start(bias[:, 6, :], dram["bg"].partition_broadcast(B)).then_inc(vec_loaded, 16)
            sp.dma_start(bias[:, 7, :], dram["bb"].partition_broadcast(B)).then_inc(vec_loaded, 16)
            for n, name in enumerate(VEC):
                sp.dma_start(vec[:, n, :], dram[name].partition_broadcast(B)).then_inc(vec_loaded, 16)
            sp.wait_ge(raw_mm, 2)
            sp.dma_start(w_style[:, :, 0, :], dram["wg_t"].rearrange("(c p) n -> p c n", p=P)).then_inc(style_loaded, 16)
            sp.dma_start(w_style[:, :, 1, :], dram["wb_t"].rearrange("(c p) n -> p c n", p=P)).then_inc(style_loaded, 16)
            next_weights.load(sp)
            sp.wait_ge(raw_done, 1)
            for row, n in RAW.items():
                sp.dma_start(mods[:, row, :], raw[:, n, :]).then_inc(table_stored, 16)
            sp.wait_ge(made_done, 7)
            for n, row in enumerate(MADE):
                sp.dma_start(mods[:, row, :], made[:, n, :]).then_inc(table_stored, 16)
            sp.wait_ge(table_stored, 160)
            for b in range(B):
                sp.dma_start(rows[24 * b:24 * b + 24, :],
                             mods[b, 0:COLS, :].rearrange("v (c p) -> (v c) p", p=P)).then_inc(rows_loaded, 16)
            sp.dma_start(rows[48:64, :], dram["b_ff1"].rearrange("(c p) -> c p", p=P)).then_inc(rows_loaded, 16)
            sp.dma_start(rows[64:68, :], dram["b_q1"].rearrange("(c p) -> c p", p=P)).then_inc(rows_loaded, 16)
            sp.dma_start(rows[68:72, :], dram["b_k1"].rearrange("(c p) -> c p", p=P)).then_inc(rows_loaded, 16)

        @block.scalar
        def _(act):
            act.wait_ge(cond_done, 1)
            act.activation(sig[:], cond[:], ACT.Exp, scale=-1.0).then_inc(exp_done, 1)
            next_weights.round_hi(act)

        @block.vector
        def _(dve):
            dve.wait_ge(cond_mm, 1)
            dve.tensor_copy(cond[:].rearrange("p b c -> p (b c)"), ps[:, 0, 0:B * C]).then_inc(cond_done, 1)
            dve.wait_ge(exp_done, 1)
            dve.tensor_scalar(sig[:], sig[:], 1.0, None, ALU.add).then_inc(sig_done, 1)
            dve.wait_ge(sig_done, 1)
            dve.reciprocal(sig[:], sig[:]).then_inc(sig_done, 1)
            dve.wait_ge(sig_done, 2)
            dve.tensor_tensor(silu[:], cond[:], sig[:], ALU.mult).then_inc(silu_done, 1)
            dve.wait_ge(raw_mm, 8)
            dve.wait_ge(vec_loaded, 144)
            dve.tensor_tensor(raw[:], ps[0:B], bias[:], ALU.add).then_inc(raw_done, 1)
            dve.wait_ge(raw_done, 1)
            dve.scalar_tensor_tensor(made[:, 0, :], raw[:, 1, :], 1.0, vec[:, 0, :], ALU.add, ALU.mult).then_inc(made_done, 1)
            dve.scalar_tensor_tensor(made[:, 1, :], raw[:, 4, :], 1.0, vec[:, 1, :], ALU.add, ALU.mult).then_inc(made_done, 1)
            dve.tensor_tensor(made[:, 4, :], raw[:, 6, :], vec[:, 4, :], ALU.mult).then_inc(made_done, 1)
            dve.tensor_tensor(made[:, 5, :], raw[:, 6, :], vec[:, 5, :], ALU.mult).then_inc(made_done, 1)
            dve.tensor_tensor(made[:, 2, :], raw[:, 2, :], vec[:, 2, :], ALU.mult).then_inc(made_done, 1)
            dve.tensor_tensor(made[:, 3, :], raw[:, 5, :], vec[:, 3, :], ALU.mult).then_inc(made_done, 1)
            dve.wait_ge(made_done, 6)
            dve.tensor_tensor(made[:, 5, :], made[:, 5, :], raw[:, 7, :], ALU.add).then_inc(made_done, 1)
            next_weights.rest_lo(dve, 0, 2)
            dve.wait_ge(cols_mm, 1)
            dve.tensor_copy(cols[:], ps[:, 0, 0:72]).then_inc(cols_done, 1)
            next_weights.rest_lo(dve, 2)
            next_weights.wait_split(dve)
            dve.wait_ge(cols_done, 1)

        @block.tensor
        def _(pe):
            pe.wait_ge(cond_loaded, 32)
            pe.transpose(ps[:, 0, 0:B * C], cond_rows[:], ident[0:B * C, 0:B * C]).then_inc(cond_mm, 1)
            pe.wait_ge(silu_done, 1)
            for n in range(8):
                if n == 6:
                    pe.wait_ge(style_loaded, 32)
                elif n < 6:
                    pe.wait_ge(ada_loaded[n], 16)
                for c in range(C):
                    lhs = silu[:, :, c] if n < 6 else cond[:, :, c]
                    rhs = w_ada[:, c, n * D:(n + 1) * D] if n < 6 else w_style[:, c, n - 6, :]
                    mm = pe.matmul(ps[0:B, n, :], lhs, rhs, start=c == 0, stop=c == C - 1)
                mm.then_inc(raw_mm, 1)
            pe.wait_ge(rows_loaded, 80)
            pe.wait_ge(raw_done, 1)
            pe.transpose(ps[:, 0, 0:72], rows[:], ident[0:72, 0:72]).then_inc(cols_mm, 1)

        inner.close()
        m.clear()


def column(cols, row, b, c):
    return cols[:, ds(b * (COLS * C) + (row * C + c), 1)]


def window_weights(m, dram):
    wqkv, wqkv_raw = m.hi_lo("wqkv", [P, C, 3 * D])
    wout, wout_raw = m.hi_lo("wout", [P, C, D])
    src = dram["w_qkv0"].rearrange("(c p) n -> p c n", p=P)
    weights = Weights(m, [(src[:, :, n * D:(n + 1) * D], *(w[:, :, n * D:(n + 1) * D] for w in (wqkv_raw, *wqkv)))
                          for n in range(3)]
                      + [(dram["w_out0"].rearrange("(c p) n -> p c n", p=P), *(w[:] for w in (wout_raw, *wout)))])
    return wqkv, wout, weights


def window_attention(nc, dram, x, x1, mods, ident, cols, wqkv, wout, next_weights, T):
    N = T // P
    WPB = N // 2
    H, DH = 8, 64
    with ExitStack() as stack:
        m = Memory(nc, stack, "win")
        bqkv = m.sb("bqkv", [P, 3, D])
        gate = m.sb("gate", [P, 2, D])
        gbias = m.sb("gbias", [P, 2, D])
        cos = m.sb("cos", [P, DH])
        sin = m.sb("sin", [P, DH])
        xw = m.sb("xw", [P, 2, D])
        sq = m.sb("sq", [P, D])
        ss = m.sb("ss", [P, 2])
        var = m.sb("var", [P, 2])
        half = m.sb("half", [P, 1])
        eps = m.sb("eps", [P, 1])
        rstd = m.sb("rstd", [P, 2])
        xn = m.sb("xn", [P, 2, D])
        hf = m.sb("hf", [P, C, P])
        hh = m.sb("hh", [P, 2, C, P], F32R)
        hl = m.sb("hl", [P, 2, C, P], F32R)
        qk = m.sb("qk", [P, 2 * D])
        rot = m.sb("rot", [P, 2 * D])
        qkr = m.sb("qkr", [P, 2 * D])
        v = m.sb("v", [P, 2, D])
        qkt = m.sb("qkt", [P, 2, C, P])
        negmax = m.sb("negmax", [P, H])
        pr = m.sb("pr", [P, H, P])
        sums = m.sb("sums", [P, H])
        rsum = m.sb("rsum", [P, H])
        prt = m.sb("prt", [P, H, P])
        o = m.sb("o", [P, D])
        oh = m.sb("oh", [P, C, P], F32R)
        ol = m.sb("ol", [P, C, P], F32R)
        gated = m.sb("gated", [P, D])
        xres = m.sb("xres", [P, 2, D])
        xo = m.sb("xo", [P, 2, D])
        ps_x = m.ps("ps_x", [P, D])
        ps_mm = m.ps("ps_mm", [P, 2, D])
        ps_t = m.ps("ps_t", [P, 2, D])
        ps_s = m.ps("ps_s", [P, 2, D])
        s = m.sem
        const_loaded, pow_set = s("const_loaded"), s("pow_set")
        x_loaded, xres_loaded, stored = ([s(f"{n}{i}") for i in range(2)] for n in ("x_loaded", "xres_loaded", "stored"))
        sq_done, var_done, rstd_done, xn_done = s("sq_done"), s("var_done"), s("rstd_done"), s("xn_done")
        xt_mm, affine_done, hh_done, hl_done = s("xt_mm"), s("affine_done"), s("hh_done"), s("hl_done")
        qkv_mm, qkv_out, rope_part, rope_done = s("qkv_mm"), s("qkv_out"), s("rope_part"), s("rope_done")
        qkt_mm, qkt_out, score_mm, max_done, exp_done = s("qkt_mm"), s("qkt_out"), s("score_mm"), s("max_done"), s("exp_done")
        prt_mm, prt_out, pv_mm, rsum_done, o_done = s("prt_mm"), s("prt_out"), s("pv_mm"), s("rsum_done"), s("o_done")
        ot_mm, oh_done, ol_done, out_mm, gated_done, xres_done, x1_done = (s(n) for n in (
            "ot_mm", "oh_done", "ol_done", "out_mm", "gated_done", "xres_done", "x1_done"))
        inner = stack.enter_context(ExitStack())
        block = inner.enter_context(nc.Block())

        STEPS, HEAD, TAIL = N + 4, 4, 4
        NEXT = TAIL

        def next_chunk(j, u):
            return 2 * j + u - (STEPS - TAIL) if isinstance(j, int) and 2 * j + u >= STEPS - TAIL else None

        def score(h):
            return ps_s[:, h % 2, (h // 2) * P:(h // 2 + 1) * P]

        @block.sync
        def _(sp):
            sp.dma_start(cos[:], dram["cos"]).then_inc(const_loaded, 16)
            sp.dma_start(sin[:], dram["sin"]).then_inc(const_loaded, 16)
            sp.dma_start(bqkv[:].rearrange("p a b -> p (a b)"), dram["b_qkv0"].partition_broadcast(P)).then_inc(const_loaded, 16)
            for b in range(2):
                sp.dma_start(gate[:, b], mods[b, GATE0].partition_broadcast(P)).then_inc(const_loaded, 16)
                sp.dma_start(gbias[:, b], mods[b, GBIAS0].partition_broadcast(P)).then_inc(const_loaded, 16)

            def step(j, u):
                w, p, _ = back(j, u, 4)
                if live(w, N):
                    wait(sp, x1_done, w + 1)
                    sp.dma_start(x1[ds(w * P, P), :], xo[:, p]).then_inc(stored[p], 16)
                w, p, _ = back(j, u, 3)
                if live(w, N):
                    wait(sp, x1_done, w - 1)
                    sp.dma_start(xres[:, p], x[ds(w * P, P), :]).then_inc(xres_loaded[p], 16)
                w, p, _ = back(j, u, 0)
                if live(w, N):
                    wait(sp, xn_done, w - 1)
                    sp.dma_start(xw[:, p], x[ds(w * P, P), :]).then_inc(x_loaded[p], 16)

            for s_ in range(HEAD):
                step(*divmod(s_, 2))
            next_weights.load(sp, 0, NEXT)
            with sp.Fori(HEAD // 2, (STEPS - TAIL) // 2) as j:
                for u in range(2):
                    step(j, u)
            for s_ in range(STEPS - TAIL, STEPS):
                step(*divmod(s_, 2))
            for p in range(2):
                sp.wait_ge(stored[p], 16 * (N // 2))

        @block.gpsimd
        def _(pool):
            pool.memset(half[:], -0.5).then_inc(pow_set, 1)
            pool.memset(eps[:], EPS).then_inc(pow_set, 1)
            pool.wait_ge(pow_set, 2)
            pool.wait_ge(const_loaded, 112)

            def step(j, u):
                w, p, _ = back(j, u, 0)
                if live(w, N):
                    wait(pool, sq_done, w + 1)
                    pool.tensor_tensor(var[:, p:p + 1], ss[:, p:p + 1], eps[:], ALU.add).then_inc(var_done, 1)
                    wait(pool, var_done, w + 1)
                    pool.tensor_tensor(rstd[:, p:p + 1], var[:, p:p + 1], half[:], ALU.pow).then_inc(rstd_done, 1)
                w, p, k = back(j, u, 3)
                if live(w, N):
                    wait(pool, xres_loaded[p], 16 * (k + 1))
                    pool.tensor_tensor(xres[:, p], xres[:, p], gbias[:, ds(w // WPB, 1), :].rearrange("p a d -> p (a d)"),
                                       ALU.add).then_inc(xres_done, 1)

            pipeline(pool, STEPS, HEAD, TAIL, step)

        @block.scalar
        def _(act):
            def step(j, u):
                n = next_chunk(j, u)
                if n is not None:
                    next_weights.round_hi(act, n, n + 1)
                w, p, _ = back(j, u, 2)
                if live(w, N):
                    for i in range(2):
                        wait(act, qkt_mm, 2 * w + 1 + i)
                        if i == 0:
                            wait(act, score_mm, w)
                        act.activation(qkt[:, i], ps_t[:, i, :].rearrange("p (c t) -> p c t", c=C), ACT.Copy,
                                       scale=0.125 if i == 0 else 1.0).then_inc(qkt_out, 1)
                w3, _, _ = back(j, u, 3)
                if live(w3, N):
                    wait(act, ot_mm, w3 + 1)
                    wait(act, out_mm, w3)
                    act.activation(oh[:], ps_s[:, 1, :].rearrange("p (c t) -> p c t", c=C), ACT.Copy).then_inc(oh_done, 1)
                w0, p0, k0 = back(j, u, 0)
                if live(w0, N):
                    wait(act, x_loaded[p0], 16 * (k0 + 1))
                    act.activation(sq[:], xw[:, p0], ACT.Square, scale=D ** -0.5, accum_out=ss[:, p0:p0 + 1]).then_inc(sq_done, 1)
                if live(w, N):
                    wait(act, max_done, w + 1)
                    for h in range(H):
                        e = act.activation(pr[:, h], score(h), ACT.Exp, bias=negmax[:, 4 * (h % 2) + h // 2:4 * (h % 2) + h // 2 + 1],
                                           accum_out=sums[:, h:h + 1])
                    e.then_inc(exp_done, 1)
                    for i in range(2):
                        wait(act, prt_mm, 2 * w + 1 + i)
                        if i == 0:
                            wait(act, pv_mm, w)
                        act.activation(prt[:, 4 * i:4 * i + 4], ps_t[:, i, :].rearrange("p (h t) -> p h t", h=4),
                                       ACT.Copy).then_inc(prt_out, 1)
                if live(w0, N):
                    wait(act, xt_mm, w0 + 1)
                    wait(act, hl_done, w0)
                    for c in range(C):
                        a = act.activation(hf[:, c], ps_x[:, c * P:(c + 1) * P], ACT.Identity,
                                           scale=column(cols, SCALE0, w0 // WPB, c), bias=column(cols, SHIFT0, w0 // WPB, c))
                    a.then_inc(affine_done, 1)

            pipeline(act, STEPS, HEAD, TAIL, step)

        @block.vector
        def _(dve):
            dve.wait_ge(const_loaded, 112)
            qk_h = qk[:].rearrange("p (h z d) -> p h z d", z=2, d=DH // 2)
            rot_h = rot[:].rearrange("p (h z d) -> p h z d", z=2, d=DH // 2)

            def step(j, u):
                n = next_chunk(j, u)
                if n is not None:
                    next_weights.rest_lo(dve, n, n + 1)
                w1, p1, _ = back(j, u, 1)
                w2, p2, _ = back(j, u, 2)
                w0, p0, _ = back(j, u, 0)
                w3, p3, k3 = back(j, u, 3)
                if live(w3, N):
                    wait(dve, oh_done, w3 + 1)
                    dve.tensor_tensor(ol[:], ps_s[:, 1, :].rearrange("p (c t) -> p c t", c=C), oh[:].bitcast(F32),
                                      ALU.subtract).then_inc(ol_done, 1)
                if live(w1, N):
                    wait(dve, qkv_mm, 3 * w1 + 1)
                    wait(dve, rope_done, w1)
                    dve.tensor_tensor(qk[:, 0:D], ps_mm[:, 0, :], bqkv[:, 0, :], ALU.add).then_inc(qkv_out, 1)
                if live(w2, N):
                    wait(dve, score_mm, w2 + 1)
                    dve.tensor_reduce(negmax[:], ps_s[:].rearrange("p a (h k) -> p (a h) k", k=P), AX.X, ALU.max,
                                      negate=True).then_inc(max_done, 1)
                if live(w1, N):
                    wait(dve, qkv_mm, 3 * w1 + 2)
                    dve.tensor_tensor(qk[:, D:2 * D], ps_mm[:, 1, :], bqkv[:, 1, :], ALU.add).then_inc(qkv_out, 1)
                if live(w0, N):
                    wait(dve, rstd_done, w0 + 1)
                    wait(dve, xt_mm, w0 - 1)
                    dve.tensor_scalar(xn[:, p0], xw[:, p0], rstd[:, p0:p0 + 1], None, ALU.mult).then_inc(xn_done, 1)
                if live(w1, N):
                    wait(dve, qkt_mm, 2 * w1)
                    wait(dve, qkv_out, 3 * w1 + 2)
                    dve.tensor_tensor(rot_h[:, :, 0, :], qk_h[:, :, 1, :],
                                      sin[:, 0:32].unsqueeze(1).to_broadcast([P, 16, 32]), ALU.mult).then_inc(rope_part, 1)
                    dve.tensor_tensor(rot_h[:, :, 1, :], qk_h[:, :, 0, :],
                                      sin[:, 32:64].unsqueeze(1).to_broadcast([P, 16, 32]), ALU.mult).then_inc(rope_part, 1)
                    dve.tensor_tensor(qkr[:].rearrange("p (h d) -> p h d", d=DH), qk[:].rearrange("p (h d) -> p h d", d=DH),
                                      cos[:].unsqueeze(1).to_broadcast([P, 16, DH]), ALU.mult).then_inc(rope_part, 1)
                    wait(dve, qkv_mm, 3 * w1 + 3)
                    wait(dve, pv_mm, w1 - 1)
                    dve.tensor_tensor(v[:, p1], ps_mm[:, 0, :], bqkv[:, 2, :], ALU.add).then_inc(qkv_out, 1)
                    wait(dve, rope_part, 3 * w1 + 3)
                    dve.tensor_tensor(qkr[:], qkr[:], rot[:], ALU.add).then_inc(rope_done, 1)
                if live(w2, N):
                    wait(dve, exp_done, w2 + 1)
                    dve.reciprocal(rsum[:], sums[:]).then_inc(rsum_done, 1)
                if live(w0, N):
                    wait(dve, affine_done, w0 + 1)
                    dve.tensor_copy(hh[:, p0], hf[:]).then_inc(hh_done, 1)
                    wait(dve, hh_done, w0 + 1)
                    dve.tensor_tensor(hl[:, p0], hf[:], hh[:, p0].bitcast(F32), ALU.subtract).then_inc(hl_done, 1)
                if live(w3, N):
                    wait(dve, out_mm, w3 + 1)
                    dve.tensor_tensor(gated[:], ps_mm[:, 1, :], gate[:, ds(w3 // WPB, 1), :].rearrange("p a d -> p (a d)"),
                                      ALU.mult).then_inc(gated_done, 1)
                if live(w2, N):
                    wait(dve, pv_mm, w2 + 1)
                    wait(dve, rsum_done, w2 + 1)
                    dve.tensor_tensor(o[:].rearrange("p (h d) -> p h d", d=DH), ps_s[:, 0, :].rearrange("p (h d) -> p h d", d=DH),
                                      rsum[:].unsqueeze(2).to_broadcast([P, H, DH]), ALU.mult).then_inc(o_done, 1)
                if live(w3, N):
                    wait(dve, gated_done, w3 + 1)
                    wait(dve, xres_done, w3 + 1)
                    wait(dve, stored[p3], 16 * k3)
                    dve.tensor_tensor(xo[:, p3], gated[:], xres[:, p3], ALU.add).then_inc(x1_done, 1)

            pipeline(dve, STEPS, HEAD, TAIL, step)

        @block.tensor
        def _(pe):
            def project(w, p, n):
                for c in range(C):
                    mm = triple(pe, ps_mm[:, n % 2, :], (hh[:, p, c, :], hl[:, p, c, :]),
                                [x_[:, c, n * D:(n + 1) * D] for x_ in wqkv], c == 0, c == C - 1)
                mm.then_inc(qkv_mm, 1)

            def step(j, u):
                w0, p0, _ = back(j, u, 0)
                w1, p1, _ = back(j, u, 1)
                w2, p2, _ = back(j, u, 2)
                w3, p3, _ = back(j, u, 3)
                if live(w2, N):
                    wait(pe, rope_done, w2 + 1)
                    wait(pe, prt_out, 2 * w2)
                    for i in range(2):
                        for c in range(C):
                            mm = pe.transpose(ps_t[:, i, c * P:(c + 1) * P], qkr[:, i * D + c * P:i * D + (c + 1) * P], ident[:])
                        mm.then_inc(qkt_mm, 1)
                if live(w3, N):
                    wait(pe, o_done, w3 + 1)
                    for c in range(C):
                        mm = pe.transpose(ps_s[:, 1, c * P:(c + 1) * P], o[:, c * P:(c + 1) * P], ident[:])
                    mm.then_inc(ot_mm, 1)
                if live(w1, N):
                    wait(pe, hl_done, w1 + 1)
                    wait(pe, qkv_out, 3 * w1)
                    project(w1, p1, 0)
                if live(w2, N):
                    wait(pe, qkt_out, 2 * w2 + 2)
                    wait(pe, o_done, w2)
                    wait(pe, ol_done, w2)
                    for h in range(H):
                        at = slice(64 * (h % 2), 64 * (h % 2) + 64)
                        mm = pe.matmul(score(h), qkt[at, 0, h // 2, :], qkt[at, 1, h // 2, :],
                                       start=True, stop=True)
                    mm.then_inc(score_mm, 1)
                if live(w1, N):
                    wait(pe, gated_done, w1 - 2)
                    project(w1, p1, 1)
                    wait(pe, qkv_out, 3 * w1 + 1)
                    project(w1, p1, 2)
                if live(w2, N):
                    wait(pe, exp_done, w2 + 1)
                    for h in range(H):
                        mm = pe.transpose(ps_t[:, h // 4, (h % 4) * P:(h % 4 + 1) * P], pr[:, h, :], ident[:])
                        if h % 4 == 3:
                            mm.then_inc(prt_mm, 1)
                if live(w0, N):
                    wait(pe, xn_done, w0 + 1)
                    wait(pe, affine_done, w0)
                    for c in range(C):
                        mm = pe.transpose(ps_x[:, c * P:(c + 1) * P], xn[:, p0, c * P:(c + 1) * P], ident[:])
                    mm.then_inc(xt_mm, 1)
                if live(w3, N):
                    wait(pe, ol_done, w3 + 1)
                    wait(pe, gated_done, w3)
                    if live(w3 + 2, N):
                        wait(pe, qkv_out, 3 * (w3 + 2) + 2)
                    for c in range(C):
                        mm = triple(pe, ps_mm[:, 1, :], (oh[:, c, :], ol[:, c, :]), [x_[:, c, :] for x_ in wout], c == 0, c == C - 1)
                    mm.then_inc(out_mm, 1)
                if live(w2, N):
                    wait(pe, prt_out, 2 * w2 + 2)
                    wait(pe, qkv_out, 3 * w2 + 3)
                    for h in range(H):
                        mm = pe.matmul(ps_s[:, 0, h * DH:(h + 1) * DH], prt[:, h, :], v[:, p2, h * DH:(h + 1) * DH],
                                       start=True, stop=True)
                    mm.then_inc(pv_mm, 1)

            pipeline(pe, STEPS, HEAD, TAIL, step)

        inner.close()
        m.clear()


def feed_forward_weights(m, dram):
    w1, w1_raw = m.hi_lo("w1", [P, C, 4 * D])
    src1 = dram["w_ff1"].rearrange("(c p) n -> p c n", p=P)
    src2 = dram["w_ff2"].rearrange("(j p) n -> p j n", p=P)
    weights = Weights(m, [(src1[:, :, n * D:(n + 1) * D], *(w[:, :, n * D:(n + 1) * D] for w in (w1_raw, *w1))) for n in range(4)]
                      + [(src2[:, 4 * n:4 * n + 4, :], None, None, None) for n in range(4)])
    return w1, weights


def feed_forward(nc, dram, x1, x2, mods, ident, cols, w1, weights, T):
    NB = T // D
    BPB = NB // 2
    F = 4 * D
    J = F // P
    K = 4
    with ExitStack() as stack:
        m = Memory(nc, stack, "ff")
        w2, w2_raw = m.hi_lo("w2", [P, J, D])
        W1_CHUNKS = 4
        weights.chunks[W1_CHUNKS:] = [(c[0], *(w[:, 4 * n:4 * n + 4, :] for w in (w2_raw, *w2)))
                                      for n, c in enumerate(weights.chunks[W1_CHUNKS:])]
        s = m.sem
        gate = m.sb("gate", [P, 2, D])
        gbias = m.sb("gbias", [P, 2, D])
        xw = m.sb("xw", [P, 2, D])
        sq = m.sb("sq", [P, D])
        ss = m.sb("ss", [P, 2])
        var = m.sb("var", [P, 2])
        half = m.sb("half", [P, 1])
        eps = m.sb("eps", [P, 1])
        rstd = m.sb("rstd", [P, 2])
        xn = m.sb("xn", [P, 2, D])
        hf = m.sb("hf", [P, 2, C, P])
        hh = m.sb("hh", [P, 2, C, K * P], F32R)
        hl = m.sb("hl", [P, 2, C, K * P], F32R)
        g = m.sb("g", [P, 2, D])
        gh = m.sb("gh", [P, 2, D], F32R)
        gl = m.sb("gl", [P, 2, D], F32R)
        xres = m.sb("xres", [P, 2, D])
        xo = m.sb("xo", [P, K, D])
        ps_x = m.ps("ps_x", [P, 2, D])
        ps_f = m.ps("ps_f", [P, 2, D])
        ps_y = m.ps("ps_y", [P, K, D])
        const_loaded, pow_set = s("const_loaded"), s("pow_set")
        x_loaded, xres_loaded, stored = ([s(f"{n}{i}") for i in range(2)] for n in ("x_loaded", "xres_loaded", "stored"))
        sq_done, var_done, rstd_done, xn_done = s("sq_done"), s("var_done"), s("rstd_done"), s("xn_done")
        xt_mm, affine_done, hh_done, hl_done = s("xt_mm"), s("affine_done"), s("hh_done"), s("hl_done")
        f1_mm, gelu_done, gh_done, gl_done, f2_mm = s("f1_mm"), s("gelu_done"), s("gh_done"), s("gl_done"), s("f2_mm")
        gated_done, xres_done, x2_done = s("gated_done"), s("xres_done"), s("x2_done")
        block = stack.enter_context(nc.Block())

        STEPS, HEAD, TAIL = NB + 1, 2, 1
        TURN = {3 * k + 3: k for k in range(K)}
        SPLIT = {(0, 15): 4, (1, 2): 5, (1, 6): 6, (1, 10): 7}

        def weights_at(b0, c_):
            n = SPLIT.get((b0, c_), None) if isinstance(b0, int) else None
            return None if n is None else (n, n + 1)

        @block.sync
        def _(sp):
            for b in range(2):
                sp.dma_start(gate[:, b], mods[b, GATE1].partition_broadcast(P)).then_inc(const_loaded, 16)
                sp.dma_start(gbias[:, b], mods[b, GBIAS1].partition_broadcast(P)).then_inc(const_loaded, 16)

            def step(j, u):
                b0, _, _ = back(j, u, 0)
                b1, _, _ = back(j, u, 1)

                def load_res(k):
                    wait(sp, x2_done, K * b1 + k - 1)
                    sp.dma_start(xres[:, k % 2], x1[ds((b1 * K + k) * P, P), :]).then_inc(xres_loaded[k % 2], 16)

                def store(k):
                    wait(sp, x2_done, K * b1 + k + 1)
                    sp.dma_start(x2[ds((b1 * K + k) * P, P), :], xo[:, k]).then_inc(stored[k % 2], 16)

                for k in range(0 if isinstance(b0, int) and b0 == 0 else 2, K + 2):
                    if live(b0, NB) and (k < K or live(b0 + 1, NB)):
                        wait(sp, xn_done, K * b0 + k - 1)
                        sp.dma_start(xw[:, k % 2], x1[ds((b0 * K + k) * P, P), :]).then_inc(x_loaded[k % 2], 16)
                    if k == K - 1 and isinstance(b0, int) and b0 == 0:
                        weights.load(sp, W1_CHUNKS)
                    if k == K - 1 and live(b1, NB):
                        load_res(0)
                        load_res(1)
                if live(b1, NB):
                    store(0)
                    load_res(2)
                    store(1)
                    load_res(3)
                    store(2)
                    store(3)

            pipeline(sp, STEPS, HEAD, TAIL + 2, step)
            for p in range(2):
                sp.wait_ge(stored[p], 16 * (K // 2) * NB)

        @block.gpsimd
        def _(pool):
            pool.memset(half[:], -0.5).then_inc(pow_set, 1)
            pool.memset(eps[:], EPS).then_inc(pow_set, 1)
            pool.wait_ge(pow_set, 2)
            pool.wait_ge(const_loaded, 64)

            def step(j, u):
                b0, _, _ = back(j, u, 0)
                b1, _, _ = back(j, u, 1)
                for k in range(K):
                    p = k % 2
                    if live(b0, NB):
                        wait(pool, sq_done, K * b0 + k + 1)
                        pool.tensor_tensor(var[:, p:p + 1], ss[:, p:p + 1], eps[:], ALU.add).then_inc(var_done, 1)
                        wait(pool, var_done, K * b0 + k + 1)
                        pool.tensor_tensor(rstd[:, p:p + 1], var[:, p:p + 1], half[:], ALU.pow).then_inc(rstd_done, 1)
                for k in range(K):
                    p = k % 2
                    if live(b1, NB):
                        wait(pool, xres_loaded[p], 16 * (2 * b1 + k // 2 + 1))
                        pool.tensor_tensor(xres[:, p], xres[:, p], gbias[:, ds(b1 // BPB, 1), :].rearrange("p a d -> p (a d)"),
                                           ALU.add).then_inc(xres_done, 1)
                        wait(pool, xres_done, K * b1 + k + 1)
                        wait(pool, gated_done, K * b1 + k + 1)
                        pool.tensor_tensor(xo[:, k], xo[:, k], xres[:, p], ALU.add).then_inc(x2_done, 1)

            pipeline(pool, STEPS, HEAD, TAIL, step)

        @block.scalar
        def _(act):
            def step(j, u):
                b0, _, _ = back(j, u, 0)
                b1, _, _ = back(j, u, 1)
                for c_ in range(J):
                    if weights_at(b0, c_):
                        weights.round_hi(act, *weights_at(b0, c_))
                    if live(b1, NB):
                        wait(act, f1_mm, J * b1 + c_ + 1)
                        wait(act, gl_done, J * b1 + c_ - 1)
                        act.activation(g[:, c_ % 2], ps_f[:, c_ % 2, :], ACT.Gelu_apprx_tanh,
                                       bias=cols[:, 48 + c_:49 + c_]).then_inc(gelu_done, 1)
                    if live(b0, NB) and c_ % 3 == (1 if live(b1, NB) else 0) and c_ // 3 < K:
                        k = c_ // 3
                        wait(act, sq_done, K * b0 + k)
                        wait(act, x_loaded[k % 2], 16 * (2 * b0 + k // 2 + 1))
                        act.activation(sq[:], xw[:, k % 2], ACT.Square, scale=D ** -0.5, accum_out=ss[:, k % 2:k % 2 + 1]).then_inc(sq_done, 1)
                    if live(b0, NB) and c_ in TURN:
                        k = TURN[c_]
                        wait(act, xt_mm, K * b0 + k + 1)
                        wait(act, hl_done, K * b0 + k - 1)
                        for c in range(C):
                            a = act.activation(hf[:, k % 2, c], ps_x[:, k % 2, c * P:(c + 1) * P], ACT.Identity,
                                               scale=column(cols, SCALE1, b0 // BPB, c), bias=column(cols, SHIFT1, b0 // BPB, c))
                        a.then_inc(affine_done, 1)

            pipeline(act, STEPS, HEAD, TAIL, step)

        @block.vector
        def _(dve):
            dve.wait_ge(const_loaded, 64)

            def step(j, u):
                b0, q0, _ = back(j, u, 0)
                b1, _, _ = back(j, u, 1)
                for c_ in range(J):
                    if weights_at(b0, c_):
                        weights.rest_lo(dve, *weights_at(b0, c_))
                    p = c_ % 2
                    if live(b0, NB) and c_ % 3 == 2 and c_ // 3 < K:
                        k = c_ // 3
                        wait(dve, rstd_done, K * b0 + k + 1)
                        wait(dve, xt_mm, K * b0 + k - 1)
                        dve.tensor_scalar(xn[:, k % 2], xw[:, k % 2], rstd[:, k % 2:k % 2 + 1], None, ALU.mult).then_inc(xn_done, 1)
                    if live(b0, NB) and c_ - 2 in TURN:
                        k = TURN[c_ - 2]
                        at = slice(k * P, (k + 1) * P)
                        wait(dve, affine_done, K * b0 + k + 1)
                        wait(dve, f1_mm, J * (b0 - 1))
                        dve.tensor_copy(hh[:, q0, :, at], hf[:, k % 2]).then_inc(hh_done, 1)
                        wait(dve, hh_done, K * b0 + k + 1)
                        dve.tensor_tensor(hl[:, q0, :, at], hf[:, k % 2], hh[:, q0, :, at].bitcast(F32),
                                          ALU.subtract).then_inc(hl_done, 1)
                    if live(b1, NB):
                        wait(dve, gelu_done, J * b1 + c_ + 1)
                        wait(dve, f2_mm, J * b1 + c_ - 1)
                        dve.tensor_copy(gh[:, p], g[:, p]).then_inc(gh_done, 1)
                        wait(dve, gh_done, J * b1 + c_ + 1)
                        dve.tensor_tensor(gl[:, p], g[:, p], gh[:, p].bitcast(F32), ALU.subtract).then_inc(gl_done, 1)
                if live(b1, NB):
                    wait(dve, f2_mm, J * b1 + J)
                    for k in range(K):
                        wait(dve, stored[k % 2], 16 * (2 * (b1 - 1) + k // 2 + 1))
                        dve.tensor_tensor(xo[:, k], ps_y[:, k, :], gate[:, ds(b1 // BPB, 1), :].rearrange("p a d -> p (a d)"),
                                          ALU.mult).then_inc(gated_done, 1)

            pipeline(dve, STEPS, HEAD, TAIL, step)

        @block.tensor
        def _(pe):
            def step(j, u):
                b0, _, _ = back(j, u, 0)
                b1, q1, _ = back(j, u, 1)
                for c_ in range(J + 1):
                    if c_ < J and live(b1, NB):
                        if c_ == 0:
                            wait(pe, hl_done, K * b1 + K)
                        wait(pe, gelu_done, J * b1 + c_ - 1)
                        for c in range(C):
                            mm = triple(pe, ps_f[:, c_ % 2, :], [w[:, c, c_ * P:(c_ + 1) * P] for w in w1],
                                        (hh[:, q1, c, :], hl[:, q1, c, :]), c == 0, c == C - 1)
                        mm.then_inc(f1_mm, 1)
                    if live(b0, NB) and c_ in TURN:
                        k = TURN[c_]
                        wait(pe, xn_done, K * b0 + k + 1)
                        wait(pe, affine_done, K * b0 + k - 1)
                        for c in range(C):
                            mm = pe.transpose(ps_x[:, k % 2, c * P:(c + 1) * P], xn[:, k % 2, c * P:(c + 1) * P], ident[:])
                        mm.then_inc(xt_mm, 1)
                    if c_ > 0 and live(b1, NB):
                        f = c_ - 1
                        wait(pe, gl_done, J * b1 + f + 1)
                        if isinstance(b1, int) and b1 == 0 and f % 4 == 0:
                            weights.wait_split(pe, W1_CHUNKS + f // 4 + 1)
                        for k in range(K):
                            if f == 0:
                                wait(pe, gated_done, K * (b1 - 1) + k + 1)
                            mm = triple(pe, ps_y[:, k, :], (gh[:, f % 2, k * P:(k + 1) * P], gl[:, f % 2, k * P:(k + 1) * P]),
                                        [w[:, f, :] for w in w2], f == 0, f == J - 1)
                        mm.then_inc(f2_mm, 1)

            pipeline(pe, STEPS, HEAD, TAIL, step)


def project_qkv(nc, dram, x2, q_hl, k_hl, v_d, ident, cols, T):
    NB = T // D
    BPB = NB // 2
    K = 4
    G = 2 * C
    with ExitStack() as stack:
        m = Memory(nc, stack, "qkv")
        w, w_raw = m.hi_lo("w", [P, C, 3 * D])
        src = dram["w_qkv1"].rearrange("(c p) n -> p c n", p=P)
        weights = Weights(m, [(src[:, :, n * D:(n + 1) * D], *(x_[:, :, n * D:(n + 1) * D] for x_ in (w_raw, *w))) for n in range(3)])
        bv = m.sb("bv", [P, D])
        xw = m.sb("xw", [P, 2, D])
        st = m.sb("st", [P, 2, 6])
        mv = m.sb("mv", [P, 2, 2])
        var = m.sb("var", [P, 2])
        half = m.sb("half", [P, 1])
        eps = m.sb("eps", [P, 1])
        rstd = m.sb("rstd", [P, 2])
        xn = m.sb("xn", [P, 2, D])
        hf = m.sb("hf", [P, 2, C, P])
        hh = m.sb("hh", [P, 2, C, K * P], F32R)
        hl = m.sb("hl", [P, 2, C, K * P], F32R)
        f = m.sb("f", [P, 2, D])
        fh = m.sb("fh", [P, 2, D], F32R)
        fl = m.sb("fl", [P, 2, D], F32R)
        vo = m.sb("vo", [P, 2, D])
        ps_x = m.ps("ps_x", [P, 2, D])
        ps_p = m.ps("ps_p", [P, 4, D])
        s = m.sem
        const_loaded, pow_set = s("const_loaded"), s("pow_set")
        x_loaded, f_stored, v_stored = ([s(f"{n}{i}") for i in range(2)] for n in ("x_loaded", "f_stored", "v_stored"))
        stat_done, mv_done, var_done, rstd_done, xn_done = (s(n) for n in ("stat_done", "mv_done", "var_done", "rstd_done", "xn_done"))
        xt_mm, affine_done, hh_done, hl_done = s("xt_mm"), s("affine_done"), s("hh_done"), s("hl_done")
        p_mm, f_done, fh_done, fl_done, v_done = s("p_mm"), s("f_done"), s("fh_done"), s("fl_done"), s("v_done")
        block = stack.enter_context(nc.Block())

        STEPS, HEAD, TAIL = NB + 1, 2, 1
        M = G + K
        TURN = {2 + 2 * k: k for k in range(K)}
        SPLIT = {(0, 9): 0, (1, 1): 1, (1, 4): 2}

        def weights_at(b0, n):
            n = SPLIT.get((b0, n)) if isinstance(b0, int) else None
            return None if n is None else (n, n + 1)

        @block.sync
        def _(sp):
            sp.dma_start(bv[:], dram["b_v1"].partition_broadcast(P)).then_inc(const_loaded, 16)

            def step(j, u):
                b0, _, _ = back(j, u, 0)
                b1, _, _ = back(j, u, 1)

                def load(k):
                    wait(sp, xn_done, K * b0 + k - 1)
                    sp.dma_start(xw[:, k % 2], x2[ds((b0 * K + k) * P, P), :]).then_inc(x_loaded[k % 2], 16)

                if isinstance(b0, int) and b0 == 0:
                    load(0)
                    load(1)
                for n in range(M):
                    if live(b0 + 1, NB) and n in (6, 8):
                        load(4 if n == 6 else 5)
                    if live(b1, NB):
                        if n < G:
                            to, c = (q_hl, n) if n < C else (k_hl, n - C)
                            wait(sp, fl_done, G * b1 + n + 1)
                            sp.dma_start(to[0, ds(b1 // BPB * D + c * P, P), ds(b1 % BPB * D, D)], fh[:, n % 2].bitcast(F32)).then_inc(f_stored[n % 2], 16)
                            sp.dma_start(to[1, ds(b1 // BPB * D + c * P, P), ds(b1 % BPB * D, D)], fl[:, n % 2].bitcast(F32)).then_inc(f_stored[n % 2], 16)
                        else:
                            k = n - G
                            wait(sp, v_done, K * b1 + k + 1)
                            sp.dma_start(v_d[ds(b1 // BPB * D, D), ds(b1 % BPB * D + k * P, P)].rearrange("(g t) f -> t g f", t=P),
                                         vo[:, k % 2].rearrange("t (g f) -> t g f", g=C)).then_inc(v_stored[k % 2], 16)
                    if live(b0, NB) and n in (1, 3):
                        load(2 if n == 1 else 3)
                        if n == 3 and isinstance(b0, int) and b0 == 0:
                            weights.load(sp)

            pipeline(sp, STEPS, HEAD, TAIL + 2, step)
            for p in range(2):
                sp.wait_ge(f_stored[p], 32 * (G // 2) * NB)
                sp.wait_ge(v_stored[p], 16 * (K // 2) * NB)

        @block.gpsimd
        def _(pool):
            pool.memset(half[:], -0.5).then_inc(pow_set, 1)
            pool.memset(eps[:], EPS).then_inc(pow_set, 1)
            pool.wait_ge(pow_set, 2)

            def step(j, u):
                b0, _, _ = back(j, u, 0)
                for k in range(K):
                    p = k % 2
                    if live(b0, NB):
                        wait(pool, mv_done, K * b0 + k + 1)
                        pool.tensor_tensor(var[:, p:p + 1], mv[:, p, 1:2], eps[:], ALU.add).then_inc(var_done, 1)
                        wait(pool, var_done, K * b0 + k + 1)
                        pool.tensor_tensor(rstd[:, p:p + 1], var[:, p:p + 1], half[:], ALU.pow).then_inc(rstd_done, 1)

            pipeline(pool, STEPS, HEAD, TAIL, step)

        @block.scalar
        def _(act):

            def step(j, u):
                b0, _, _ = back(j, u, 0)
                b1, _, _ = back(j, u, 1)
                for n in range(M):
                    if weights_at(b0, n):
                        weights.round_hi(act, *weights_at(b0, n))
                    if live(b1, NB) and n < G:
                        wait(act, p_mm, M * b1 + n + 1)
                        wait(act, fl_done, G * b1 + n - 1)
                        act.activation(f[:, n % 2], ps_p[:, n % 4, :], ACT.Identity, bias=cols[:, 64 + n:65 + n]).then_inc(f_done, 1)
                    if live(b0, NB) and n in TURN:
                        k = TURN[n]
                        wait(act, xt_mm, K * b0 + k + 1)
                        wait(act, hl_done, K * b0 + k - 1)
                        for c in range(C):
                            a = act.activation(hf[:, k % 2, c], ps_x[:, k % 2, c * P:(c + 1) * P], ACT.Identity,
                                               scale=column(cols, SCALE2, b0 // BPB, c), bias=column(cols, SHIFT2, b0 // BPB, c))
                        a.then_inc(affine_done, 1)

            pipeline(act, STEPS, HEAD, TAIL, step)

        @block.vector
        def _(dve):
            dve.wait_ge(const_loaded, 16)

            def step(j, u):
                b0, q0, _ = back(j, u, 0)
                b1, _, _ = back(j, u, 1)

                def stats(k):
                    p = k % 2
                    wait(dve, x_loaded[p], 16 * (2 * b0 + k // 2 + 1))
                    dve.bn_stats(st[:, p], xw[:, p]).then_inc(stat_done, 1)
                    wait(dve, stat_done, K * b0 + k + 1)
                    wait(dve, rstd_done, K * b0 + k - 1)

                def aggregate(k):
                    p = k % 2
                    dve.bn_aggr(mv[:, p], st[:, p]).then_inc(mv_done, 1)

                def normalise(k):
                    p = k % 2
                    wait(dve, mv_done, K * b0 + k + 1)
                    wait(dve, rstd_done, K * b0 + k + 1)
                    wait(dve, xt_mm, K * b0 + k - 1)
                    dve.tensor_scalar(xn[:, p], xw[:, p], mv[:, p, 0:1], rstd[:, p:p + 1], ALU.subtract, ALU.mult).then_inc(xn_done, 1)

                for n in range(M):
                    if weights_at(b0, n):
                        weights.rest_lo(dve, *weights_at(b0, n))
                    if live(b0, NB) and n % 2 == 0 and n // 2 < K:
                        stats(n // 2)
                    if live(b0, NB) and n % 2 == 1 and n // 2 < K:
                        normalise(n // 2)
                    if live(b0, NB) and n - 1 in TURN:
                        k = TURN[n - 1]
                        at = slice(k * P, (k + 1) * P)
                        wait(dve, affine_done, K * b0 + k + 1)
                        wait(dve, p_mm, M * (b0 - 1))
                        dve.tensor_copy(hh[:, q0, :, at], hf[:, k % 2]).then_inc(hh_done, 1)
                        wait(dve, hh_done, K * b0 + k + 1)
                        dve.tensor_tensor(hl[:, q0, :, at], hf[:, k % 2], hh[:, q0, :, at].bitcast(F32),
                                          ALU.subtract).then_inc(hl_done, 1)
                    if live(b1, NB) and n < G:
                        p = n % 2
                        wait(dve, f_done, G * b1 + n + 1)
                        wait(dve, f_stored[p], 32 * ((G // 2) * b1 + n // 2))
                        dve.tensor_copy(fh[:, p], f[:, p]).then_inc(fh_done, 1)
                        wait(dve, fh_done, G * b1 + n + 1)
                        dve.tensor_tensor(fl[:, p], f[:, p], fh[:, p].bitcast(F32), ALU.subtract).then_inc(fl_done, 1)
                    if live(b1, NB) and n >= G:
                        k = n - G
                        wait(dve, p_mm, M * b1 + n + 1)
                        wait(dve, v_stored[k % 2], 16 * (2 * b1 + k // 2))
                        dve.tensor_tensor(vo[:, k % 2], ps_p[:, n % 4, :], bv[:], ALU.add).then_inc(v_done, 1)
                    if live(b0, NB) and n % 2 == 0 and n // 2 < K:
                        aggregate(n // 2)

            pipeline(dve, STEPS, HEAD, TAIL, step)

        @block.tensor
        def _(pe):
            def step(j, u):
                b0, _, _ = back(j, u, 0)
                b1, q1, _ = back(j, u, 1)
                for n in range(M):
                    if live(b1, NB):
                        if n == 0:
                            wait(pe, hl_done, K * b1 + K)
                        if isinstance(b1, int) and b1 == 0 and n % C == 0:
                            weights.wait_split(pe, n // C + 1)
                        if n < 4:
                            wait(pe, v_done, K * (b1 - 1) + n + 1)
                        else:
                            wait(pe, f_done, G * b1 + n - 3)
                        for c in range(C):
                            if n < G:
                                mm = triple(pe, ps_p[:, n % 4, :], [x_[:, c, n * P:(n + 1) * P] for x_ in w],
                                            (hh[:, q1, c, :], hl[:, q1, c, :]), c == 0, c == C - 1)
                            else:
                                at = slice((n - G) * P, (n - G + 1) * P)
                                mm = triple(pe, ps_p[:, n % 4, :], (hh[:, q1, c, at], hl[:, q1, c, at]),
                                            [x_[:, c, 2 * D:3 * D] for x_ in w], c == 0, c == C - 1)
                        mm.then_inc(p_mm, 1)
                    if live(b0, NB) and n in TURN:
                        k = TURN[n]
                        wait(pe, xn_done, K * b0 + k + 1)
                        wait(pe, affine_done, K * b0 + k - 1)
                        for c in range(C):
                            mm = pe.transpose(ps_x[:, k % 2, c * P:(c + 1) * P], xn[:, k % 2, c * P:(c + 1) * P], ident[:])
                        mm.then_inc(xt_mm, 1)

            pipeline(pe, STEPS, HEAD, TAIL, step)


def full_attention(nc, ident_src, q_hl, k_hl, v_d, o_t, next_weights, T):
    HG, HD = 4, 32
    S = T // 2
    KT = S // P
    QB = S // D
    ITEMS = 2 * C * QB
    U = KT * HG
    RING = 4
    BANKS = 3
    BANK = [n % BANKS for n in range(U - 4)] + [0, 1, 2, 1]
    LAST = [max(i for i in range(-U, n) if BANK[i % U] == BANK[n]) for n in range(U)]
    EARLY = {14: 4, 15: 4}
    AHEAD = [5, 5, 3, 2, 3, 5, 4, 4, 6, 4, 5, 6, 4, 0, 0, 0]
    SPLIT = 5
    TURN = 13
    first_block = sum(EARLY.values())
    AHEAD_AT = [first_block + sum(AHEAD[:k]) for k in range(KT + 1)]
    EARLY_AT = {k: sum(EARLY[i] for i in EARLY if i < k) for k in EARLY}
    assert AHEAD_AT[KT] == U
    PE_SUMS = (4, 7, 10, 12, 15)
    POOL_SUMS = [k for k in range(KT) if k not in PE_SUMS]
    POOL_OPS = len(POOL_SUMS) - 1
    pool_after = {k: max(n, 1) for n, k in enumerate(POOL_SUMS)}
    LOOP = 8

    def count(item, per_item, done):
        return per_item * item + (done + per_item)

    with ExitStack() as stack:
        m = Memory(nc, stack, "att")
        kst = [m.sb(f"kst{n}", [98, HG, S], F32R) for n in range(2)]
        qst = [m.sb(f"qst{n}", [98, HG, D], F32R) for n in range(4)]
        vt = [m.sb(f"vt{n}", [P, KT, HG * HD]) for n in range(2)]
        prob = m.sb("prob", [P, RING, HG, D])
        acc = m.sb("acc", [P, 2, HG, D])
        scale = m.sb("scale", [P, HD])
        mx = m.sb("mx", [P, U])
        m16 = m.sb("m16", [P, 16])
        ident = m.sb("ident", [P, P])
        nmh = m.sb("nmh", [16, 2, P], F32R)
        nml = m.sb("nml", [16, 2, P], F32R)
        oraw = m.sb("oraw", [P, D])
        rec = m.sb("rec", [P, D])
        on = m.sb("on", [P, D])
        ps_st = m.ps("ps_st", [P, BANKS, D])
        ps_mx = m.ps("ps_mx", [P, BANKS, D])
        ps_o = m.ps("ps_o", [P, D])
        ps_sum = m.ps("ps_sum", [P, D])
        s = m.sem
        const_done, ident_loaded, o_stored = s("const_done"), s("ident_loaded"), s("o_stored")
        q_loaded = [s(f"q_loaded{n}") for n in range(4)]
        k_first = [s(f"k_first{h}") for h in range(HG - 1)]
        k_loaded, v_loaded, negmax_loaded = ([s(f"{x}{n}") for n in range(2)] for x in ("k_loaded", "v_loaded", "negmax_loaded"))
        ahead_mm, max_done, allmax_done, allmax_mm, negmax_done = (s(n) for n in (
            "ahead_mm", "max_done", "allmax_done", "allmax_mm", "negmax_done"))
        half_max = s("half_max")
        score_mm, exp_done, pv_mm, pool_done, sum_mm, rec_done, oraw_done, on_done = (s(n) for n in (
            "score_mm", "exp_done", "pv_mm", "pool_done", "sum_mm", "rec_done", "oraw_done", "on_done"))
        block = stack.enter_context(nc.Block())

        def drive(eng, ahead, tile, flush):
            ahead()
            for kt in range(SPLIT):
                tile(0, 0, kt)
            with eng.Fori(0, ITEMS // LOOP - 1) as j:
                for r in range(LOOP):
                    for kt in range(SPLIT, KT):
                        tile(j, r, kt)
                    for kt in range(SPLIT):
                        tile(j, r + 1, kt)
            j = ITEMS // LOOP - 1
            for r in range(LOOP):
                for kt in range(SPLIT, KT):
                    tile(j, r, kt)
                if r + 1 < LOOP:
                    for kt in range(SPLIT):
                        tile(j, r + 1, kt)
            flush()

        @block.sync
        def _(sp):
            def load_q(j, r):
                n = 2 * j + r // QB
                for row, part in ((0, 0), (1, 1), (2, 0)):
                    sp.dma_start(qst[r % 4][HD * row:HD * row + HD].bitcast(F32),
                                 q_hl[part, ds(n * P, P), r % QB * D:(r % QB + 1) * D].rearrange(
                                     "(h d) t -> d h t", d=HD)).then_inc(q_loaded[r % 4], 16)

            def load_kv(j, r):
                n = 2 * j + r // QB
                p = (r // QB) % 2
                if isinstance(n, int) and n == 0:
                    for h in range(HG):
                        for row, part in ((0, 0), (1, 0), (2, 1)):
                            sp.dma_start(kst[p][HD * row:HD * row + HD, h].bitcast(F32), k_hl[part, HD * h:HD * h + HD, :]
                                         ).then_inc(k_first[h] if h < HG - 1 else k_loaded[p], 16)
                for row, part in ((0, 0), (1, 0), (2, 1)) if not (isinstance(n, int) and n == 0) else ():
                    sp.dma_start(kst[p][HD * row:HD * row + HD].bitcast(F32),
                                 k_hl[part, ds(n * P, P), :].rearrange(
                                     "(h d) t -> d h t", d=HD)).then_inc(k_loaded[p], 16)
                sp.dma_start(vt[p][:].rearrange("p k f -> p (k f)"), v_d[ds(n * P, P), :]).then_inc(v_loaded[p], 16)

            def load_negmax(j, r):
                wait(sp, negmax_done, count(LOOP * j + r, 1, 1))
                for row, t in ((96, nmh), (97, nml)):
                    sp.dma_start(qst[r % 4][row:row + 1].bitcast(F32).rearrange("o h (t q) -> o (h t) q", q=P),
                                 t[:, r % 2, :].bitcast(F32)).then_inc(negmax_loaded[r % 2], 16)

            def store(j, r):
                item = LOOP * j + r
                n = 2 * j + r // QB
                wait(sp, on_done, count(item, 1, 1))
                sp.dma_start(o_t[ds(n * P, P), r % QB * D:(r % QB + 1) * D], on[:]).then_inc(o_stored, 16)

            def ahead():
                sp.dma_start(ident[:], ident_src).then_inc(ident_loaded, 16)
                load_q(0, 0)
                load_kv(0, 0)
                load_q(0, 1)
                load_negmax(0, 0)
                next_weights.load(sp)

            def tile(j, r, kt):
                item = LOOP * j + r
                if kt == 3 and not (isinstance(item, int) and item == 0):
                    store(j, r - 1)
                if kt == 4:
                    wait(sp, score_mm, count(item, U, 0))
                    wait(sp, pv_mm, count(item, KT, 0))
                    if r % QB == 0 and live(item + QB, ITEMS):
                        load_kv(j, r + QB)
                    if live(item + 2, ITEMS):
                        load_q(j, r + 2)
                if kt == TURN and live(item + 1, ITEMS):
                    load_negmax(j, r + 1)

            def flush():
                store(ITEMS // LOOP - 1, LOOP - 1)
                sp.wait_ge(o_stored, 16 * ITEMS)

            drive(sp, ahead, tile, flush)

        @block.gpsimd
        def _(pool):
            pool.sem_inc(pool_done, POOL_OPS)
            pool.memset(scale[:], float(D) ** 0.5).then_inc(const_done, 1)
            for n in range(2):
                pool.wait_ge(const_done, n + 1)
                pool.memset(kst[n][96:98].bitcast(F32), 1.0).then_inc(const_done, 1)

            def tile(j, r, kt):
                item = LOOP * j + r
                if kt in POOL_SUMS and kt != POOL_SUMS[0]:
                    wait(pool, exp_done, count(item, U, HG * (kt + 1)))
                    a = acc[:, r % 2]
                    if kt == POOL_SUMS[1]:
                        wait(pool, sum_mm, count(item - 2, 1, 1))
                        first = prob[:, POOL_SUMS[0] % RING]
                    else:
                        wait(pool, pool_done, count(item, POOL_OPS, pool_after[kt] - 1))
                        first = a
                    pool.tensor_tensor(a, first, prob[:, kt % RING], ALU.add).then_inc(pool_done, 1)

            drive(pool, lambda: None, tile, lambda: None)

        @block.scalar
        def _(act):
            act.sem_inc(exp_done, U)
            act.sem_inc(oraw_done, 1)

            def copy_out(j, r):
                item = LOOP * j + r
                wait(act, pv_mm, count(item, KT, KT))
                wait(act, on_done, count(item - 1, 1, 1))
                act.activation(oraw[:], ps_o[:], ACT.Copy).then_inc(oraw_done, 1)

            def tile(j, r, kt):
                item = LOOP * j + r
                for h in range(HG):
                    wait(act, score_mm, count(item, U, HG * kt + h + 1))
                    if h == 0:
                        wait(act, pv_mm, count(item, KT, kt - RING + 1))
                        old = (kt - RING) % KT
                        if old in POOL_SUMS:
                            of = item if kt >= RING else item - 1
                            wait(act, pool_done, count(of, POOL_OPS, pool_after[old]))
                    act.activation(prob[:, kt % RING, h], ps_st[:, BANK[HG * kt + h], :], ACT.Exp).then_inc(exp_done, 1)
                    if kt == 0 and h == 3 and not (isinstance(item, int) and item == 0):
                        copy_out(j, r - 1)

            def flush():
                copy_out(ITEMS // LOOP - 1, LOOP - 1)
                next_weights.round_hi(act)

            drive(act, lambda: None, tile, flush)

        @block.vector
        def _(dve):
            for sem, n in ((max_done, U), (allmax_done, 1), (negmax_done, 1), (rec_done, 2), (on_done, 1)):
                dve.sem_inc(sem, n)

            def reduce_blocks(j, r, a, b):
                item = LOOP * j + r
                for n in range(a, b):
                    wait(dve, ahead_mm, count(item, U, n + 1))
                    if n == 0:
                        wait(dve, allmax_done, count(item, 1, 0))
                    dve.tensor_reduce(mx[:, n:n + 1], ps_mx[:, BANK[n], :], AX.X, ALU.max).then_inc(max_done, 1)
                    if n == U - 1:
                        wait(dve, max_done, count(item, U, U))
                        wait(dve, allmax_mm, item)
                        dve.tensor_reduce(m16[:], mx[:].rearrange("p (b k) -> p b k", b=16), AX.X, ALU.max,
                                          negate=True).then_inc(allmax_done, 1)

            def split_max(j, r):
                item = LOOP * j + r
                wait(dve, allmax_mm, item + 1)
                wait(dve, negmax_loaded[r % 2], 32 * (4 * j + r // 2))
                dve.tensor_copy(nmh[:, r % 2], ps_mx[0:16, 1, 0:P]).then_inc(half_max, 1)
                wait(dve, half_max, item + 1)
                dve.tensor_tensor(nml[:, r % 2], ps_mx[0:16, 1, 0:P], nmh[:, r % 2].bitcast(F32), ALU.subtract).then_inc(negmax_done, 1)

            def finish(j, r, part):
                item = LOOP * j + r
                if part < 2:
                    at = slice(part * D // 2, (part + 1) * D // 2)
                    if part == 0:
                        wait(dve, sum_mm, count(item, 1, 1))
                        wait(dve, on_done, count(item, 1, 0))
                    dve.reciprocal(rec[:, at], ps_sum[:, at]).then_inc(rec_done, 1)
                else:
                    wait(dve, rec_done, count(item, 2, 2))
                    wait(dve, oraw_done, count(item, 1, 1))
                    wait(dve, o_stored, 16 * item)
                    dve.tensor_tensor(on[:], oraw[:], rec[:], ALU.mult).then_inc(on_done, 1)

            def ahead():
                reduce_blocks(0, 0, 0, U)
                split_max(0, 0)
                reduce_blocks(0, 1, 0, first_block)

            def tile(j, r, kt):
                item = LOOP * j + r
                if live(item + 1, ITEMS):
                    reduce_blocks(j, r + 1, AHEAD_AT[kt], AHEAD_AT[kt + 1])
                    if kt == TURN:
                        split_max(j, r + 1)
                if kt in EARLY and live(item + 2, ITEMS):
                    reduce_blocks(j, r + 2, EARLY_AT[kt], EARLY_AT[kt] + EARLY[kt])
                if kt in (2, 3, 4) and not (isinstance(item, int) and item == 0):
                    finish(j, r - 1, kt - 2)

            def flush():
                for part in range(3):
                    finish(ITEMS // LOOP - 1, LOOP - 1, part)
                next_weights.rest_lo(dve)
                next_weights.wait_split(dve)

            drive(dve, ahead, tile, flush)

        @block.tensor
        def _(pe):
            for sem, n in ((ahead_mm, U), (score_mm, U), (pv_mm, KT), (sum_mm, 1)):
                pe.sem_inc(sem, n)
            pe.wait_ge(ident_loaded, 16)

            def blocks(j, r, a, b):
                item = LOOP * j + r
                for n in range(a, b):
                    if isinstance(item, int) and item == 0 and n % 16 == 0 and n // 16 < HG - 1:
                        wait(pe, k_first[n // 16], 48)
                    if n == 0:
                        wait(pe, q_loaded[r % 4], 48 * (2 * j + r // 4 + 1))
                    if n == 0 and not (isinstance(item, int) and item == 0) or isinstance(item, int) and item == 0 and n == 48:
                        wait(pe, k_loaded[(r // QB) % 2], 48 * (j + r // (2 * QB) + 1))
                    if n == 0:
                        wait(pe, allmax_done, count(item, 1, 0))
                    if n == 1:
                        wait(pe, negmax_done, count(item, 1, 0))
                    wait(pe, max_done, count(item, U, LAST[n] + 1))
                    h, t, k = n // 16, (n // 4) % 4, n % 4
                    pe.matmul(ps_mx[:, BANK[n], :], qst[r % 4][0:96, h, t * P:(t + 1) * P],
                              kst[(r // QB) % 2][0:96, h, k * D:(k + 1) * D], start=True, stop=True).then_inc(ahead_mm, 1)

            def turn_max(j, r):
                item = LOOP * j + r
                wait(pe, allmax_done, count(item, 1, 1))
                pe.transpose(ps_mx[0:16, 1, 0:P], m16[:], ident[:]).then_inc(allmax_mm, 1)

            def score(j, r, kt, h):
                item = LOOP * j + r
                n = HG * kt + h
                if n == 0:
                    wait(pe, negmax_loaded[r % 2], 32 * (4 * j + r // 2 + 1))
                wait(pe, exp_done, count(item, U, LAST[n] + 1))
                pe.matmul(ps_st[:, BANK[n], :], kst[(r // QB) % 2][:, h, kt * P:(kt + 1) * P], qst[r % 4][:, h, :],
                          start=True, stop=True).then_inc(score_mm, 1)

            def add_sums(rhs, start, stop):
                for h in range(HG):
                    mm = pe.matmul(ps_sum[HD * h:HD * h + HD, :], scale[:], rhs[:, h, :], start=start, stop=stop,
                                   skip_group_check=True)
                return mm

            def sums(j, r, kt):
                item = LOOP * j + r
                wait(pe, exp_done, count(item, U, HG * (kt + 1)))
                if kt == PE_SUMS[0]:
                    wait(pe, rec_done, count(item, 2, 0))
                add_sums(prob[:, kt % RING], kt == PE_SUMS[0], False)

            def values(j, r, kt):
                item = LOOP * j + r
                p = (r // QB) % 2
                wait(pe, exp_done, count(item, U, HG * (kt + 1)))
                if kt == 0:
                    wait(pe, oraw_done, count(item, 1, 0))
                    wait(pe, v_loaded[p], 16 * (j + r // (2 * QB) + 1))
                for h in range(HG):
                    mm = pe.matmul(ps_o[HD * h:HD * h + HD, :], vt[p][:, kt, HD * h:HD * h + HD], prob[:, kt % RING, h, :],
                                   start=kt == 0, stop=kt == KT - 1, skip_group_check=True)
                mm.then_inc(pv_mm, 1)

            def finish(j, r):
                wait(pe, pool_done, count(LOOP * j + r, POOL_OPS, POOL_OPS))
                add_sums(acc[:, r % 2], False, True).then_inc(sum_mm, 1)

            def ahead():
                blocks(0, 0, 0, U)
                turn_max(0, 0)
                blocks(0, 1, 0, first_block)
                pe.wait_ge(const_done, 3)

            def tile(j, r, kt):
                item = LOOP * j + r
                first = isinstance(item, int) and item == 0
                if kt in EARLY:
                    of, a, b = r + 2, EARLY_AT[kt], EARLY_AT[kt] + EARLY[kt]
                else:
                    of, a, b = r + 1, AHEAD_AT[kt], AHEAD_AT[kt + 1]
                if not live(LOOP * j + of, ITEMS):
                    a = b
                old_r, old_kt = (r, kt - 1) if kt > 0 else (r - 1, KT - 1)
                summed = old_kt in PE_SUMS and not (first and kt == 0)
                slots = [0, 4, 1, 5, 3, 2] if summed or kt == 2 else [0, 4, 1, 5, 3, 3]
                cut = [a]
                for slot in range(6):
                    cut.append(cut[-1] + slots[:b - a].count(slot))
                assert cut[-1] == b
                score(j, r, kt, 0)
                blocks(j, of, cut[0], cut[1])
                score(j, r, kt, 1)
                blocks(j, of, cut[1], cut[2])
                if summed:
                    sums(j, old_r, old_kt)
                if kt == 2 and not first:
                    finish(j, r - 1)
                blocks(j, of, cut[2], cut[3])
                if kt > 0 or not first:
                    values(j, old_r, old_kt)
                blocks(j, of, cut[3], cut[4])
                if kt == TURN and live(item + 1, ITEMS):
                    turn_max(j, r + 1)
                score(j, r, kt, 2)
                blocks(j, of, cut[4], cut[5])
                score(j, r, kt, 3)
                blocks(j, of, cut[5], cut[6])

            def flush():
                sums(ITEMS // LOOP - 1, LOOP - 1, KT - 1)
                values(ITEMS // LOOP - 1, LOOP - 1, KT - 1)
                finish(ITEMS // LOOP - 1, LOOP - 1)

            drive(pe, ahead, tile, flush)


def output_weights(m, dram):
    w, w_raw = m.hi_lo("w", [P, C, D])
    return w, Weights(m, [(dram["wp_t"].rearrange("(c p) n -> p c n", p=P), *(x_[:] for x_ in (w_raw, *w)))])


def output(nc, dram, o_t, x2, out, mods, w, T):
    N = T // P
    WPB = N // 2
    with ExitStack() as stack:
        m = Memory(nc, stack, "out")
        bp = m.sb("bp", [P, D])
        scale = m.sb("scale", [P, 2, D])
        shift = m.sb("shift", [P, 2, D])
        ot = m.sb("ot", [P, 2, C, P])
        oh = m.sb("oh", [P, 2, C, P], F32R)
        ol = m.sb("ol", [P, 2, C, P], F32R)
        xres = m.sb("xres", [P, 2, D])
        h1 = m.sb("h1", [P, 2, D])
        hs = m.sb("hs", [P, 2, D])
        st = m.sb("st", [P, 2, 6])
        mv = m.sb("mv", [P, 2, 2])
        var = m.sb("var", [P, 2])
        half = m.sb("half", [P, 1])
        eps = m.sb("eps", [P, 1])
        rstd = m.sb("rstd", [P, 2])
        ln = m.sb("ln", [P, 2, D])
        y = m.sb("y", [P, 2, D])
        ps = m.ps("ps", [P, 2, D])
        s = m.sem
        const_loaded, pow_set = s("const_loaded"), s("pow_set")
        o_loaded, xres_loaded, stored = ([s(f"{x_}{n}") for n in range(2)] for x_ in ("o_loaded", "xres_loaded", "stored"))
        oh_done, ol_done, mm_done, xres_done, h1_done, stat_done, mv_done, var_done, rstd_done, ln_done, hs_done, y_done = (
            s(n) for n in ("oh_done", "ol_done", "mm_done", "xres_done", "h1_done", "stat_done", "mv_done", "var_done",
                           "rstd_done", "ln_done", "hs_done", "y_done"))
        block = stack.enter_context(nc.Block())
        STEPS, HEAD, TAIL = N + 4, 4, 4

        def of_batch(t, w_):
            return t[:, ds(w_ // WPB, 1), :].rearrange("p a d -> p (a d)")

        @block.sync
        def _(sp):
            sp.dma_start(bp[:], dram["b_p"].partition_broadcast(P)).then_inc(const_loaded, 16)
            for b in range(2):
                sp.dma_start(scale[:, b], mods[b, SCALE2].partition_broadcast(P)).then_inc(const_loaded, 16)
                sp.dma_start(shift[:, b], mods[b, SHIFT2].partition_broadcast(P)).then_inc(const_loaded, 16)

            def step(j, u):
                w0, p0, _ = back(j, u, 0)
                if live(w0, N):
                    wait(sp, ol_done, w0 - 1)
                    sp.dma_start(ot[:, p0], o_t[ds(w0 // WPB * D, D), ds(w0 % WPB * P, P)].rearrange("(c p) t -> p c t", p=P)).then_inc(o_loaded[p0], 16)
                    wait(sp, h1_done, w0 - 1)
                    sp.dma_start(xres[:, p0], x2[ds(w0 * P, P), :]).then_inc(xres_loaded[p0], 16)
                w4, p4, _ = back(j, u, 4)
                if live(w4, N):
                    wait(sp, y_done, w4 + 1)
                    sp.dma_start(out[ds(w4 * P, P), :], y[:, p4]).then_inc(stored[p4], 16)

            pipeline(sp, STEPS, HEAD, TAIL, step)
            for p in range(2):
                sp.wait_ge(stored[p], 16 * (N // 2))

        @block.gpsimd
        def _(pool):
            pool.memset(half[:], -0.5).then_inc(pow_set, 1)
            pool.memset(eps[:], EPS).then_inc(pow_set, 1)
            pool.wait_ge(pow_set, 2)
            pool.wait_ge(const_loaded, 80)

            def step(j, u):
                w1, p1, k1 = back(j, u, 1)
                w2, p2, _ = back(j, u, 2)
                if live(w1, N):
                    wait(pool, xres_loaded[p1], 16 * (k1 + 1))
                    pool.tensor_tensor(xres[:, p1], xres[:, p1], bp[:], ALU.add).then_inc(xres_done, 1)
                if live(w2, N):
                    wait(pool, mv_done, w2 + 1)
                    pool.tensor_tensor(var[:, p2:p2 + 1], mv[:, p2, 1:2], eps[:], ALU.add).then_inc(var_done, 1)
                    wait(pool, var_done, w2 + 1)
                    pool.tensor_tensor(rstd[:, p2:p2 + 1], var[:, p2:p2 + 1], half[:], ALU.pow).then_inc(rstd_done, 1)
                if live(w2, N):
                    wait(pool, y_done, w2 - 1)
                    pool.tensor_tensor(hs[:, p2], h1[:, p2], of_batch(shift, w2), ALU.add).then_inc(hs_done, 1)

            pipeline(pool, STEPS, HEAD, TAIL, step)

        @block.scalar
        def _(act):
            def step(j, u):
                w1, p1, k1 = back(j, u, 1)
                if live(w1, N):
                    wait(act, o_loaded[p1], 16 * (k1 + 1))
                    wait(act, mm_done, w1 - 1)
                    act.activation(oh[:, p1], ot[:, p1], ACT.Copy).then_inc(oh_done, 1)

            pipeline(act, STEPS, HEAD, TAIL, step)

        @block.vector
        def _(dve):
            dve.wait_ge(const_loaded, 80)

            def step(j, u):
                w1, p1, _ = back(j, u, 1)
                w2, p2, _ = back(j, u, 2)
                w3, p3, k3 = back(j, u, 3)
                if live(w1, N):
                    wait(dve, oh_done, w1 + 1)
                    wait(dve, mm_done, w1 - 1)
                    dve.tensor_tensor(ol[:, p1], ot[:, p1], oh[:, p1].bitcast(F32), ALU.subtract).then_inc(ol_done, 1)
                if live(w2, N):
                    wait(dve, mm_done, w2 + 1)
                    wait(dve, xres_done, w2 + 1)
                    wait(dve, hs_done, w2 - 1)
                    dve.tensor_tensor(h1[:, p2], ps[:, p2, :], xres[:, p2], ALU.add).then_inc(h1_done, 1)
                if live(w3, N):
                    wait(dve, mv_done, w3 + 1)
                    dve.scalar_tensor_tensor(ln[:, p3], h1[:, p3], mv[:, p3, 0:1], of_batch(scale, w3), ALU.subtract, ALU.mult).then_inc(ln_done, 1)
                if live(w2, N):
                    wait(dve, h1_done, w2 + 1)
                    dve.bn_stats(st[:, p2], h1[:, p2]).then_inc(stat_done, 1)
                    wait(dve, stat_done, w2 + 1)
                if live(w3, N):
                    wait(dve, rstd_done, w3 + 1)
                    wait(dve, ln_done, w3 + 1)
                    wait(dve, hs_done, w3 + 1)
                    wait(dve, stored[p3], 16 * k3)
                    dve.scalar_tensor_tensor(y[:, p3], ln[:, p3], rstd[:, p3:p3 + 1], hs[:, p3], ALU.mult, ALU.add).then_inc(y_done, 1)
                if live(w2, N):
                    dve.bn_aggr(mv[:, p2], st[:, p2]).then_inc(mv_done, 1)

            pipeline(dve, STEPS, HEAD, TAIL, step)

        @block.tensor
        def _(pe):
            def step(j, u):
                w1, p1, _ = back(j, u, 1)
                if live(w1, N):
                    wait(pe, ol_done, w1 + 1)
                    wait(pe, h1_done, w1 - 1)
                    for c in range(C):
                        mm = triple(pe, ps[:, p1, :], (oh[:, p1, c], ol[:, p1, c]), [x_[:, c, :] for x_ in w], c == 0, c == C - 1)
                    mm.then_inc(mm_done, 1)

            pipeline(pe, STEPS, HEAD, TAIL, step)


def build(nc, dram, out):
    nc.disable_value_cache = True
    T = out.shape[0]
    x1 = nc.dram_tensor("x1", [T, D], F32, kind="Internal").ap()
    x2 = nc.dram_tensor("x2", [T, D], F32, kind="Internal").ap()
    mods = nc.dram_tensor("mods", [2, MODS, D], F32, kind="Internal").ap()
    q_hl = nc.dram_tensor("q_hl", [2, 2 * D, T // 2], F32, kind="Internal").ap()
    k_hl = nc.dram_tensor("k_hl", [2, 2 * D, T // 2], F32, kind="Internal").ap()
    v_d = nc.dram_tensor("v_d", [2 * D, T // 2], F32, kind="Internal").ap()
    o_t = nc.dram_tensor("o_t", [2 * D, T // 2], F32, kind="Internal").ap()
    with nc.sbuf_tensor("ident", [P, P], F32) as ident, nc.sbuf_tensor("cols", [P, 72], F32) as cols:
        with ExitStack() as stack:
            ff = Memory(nc, stack, "ffw")
            w1, ff_weights = feed_forward_weights(ff, dram)
            with ExitStack() as stack:
                win = Memory(nc, stack, "winw")
                wqkv, wout, win_weights = window_weights(win, dram)
                modulation(nc, dram, mods, ident, cols, win_weights)
                window_attention(nc, dram, dram["x"], x1, mods, ident, cols, wqkv, wout, ff_weights, T)
                win.clear()
            feed_forward(nc, dram, x1, x2, mods, ident, cols, w1, ff_weights, T)
        project_qkv(nc, dram, x2, q_hl, k_hl, v_d, ident, cols, T)
    with ExitStack() as stack:
        wp, out_weights = output_weights(Memory(nc, stack, "outw"), dram)
        full_attention(nc, dram["ident"], q_hl, k_hl, v_d, o_t, out_weights, T)
        output(nc, dram, o_t, x2, out, mods, wp, T)


def kernel(**inputs):
    import numpy as np
    import concourse.bacc as bacc
    from concourse.bass_utils import run_bass_kernel_spmd

    x = np.asarray(inputs["x"])
    B, L, _ = x.shape
    DH = 64
    freqs = (1.0 / 10000.0 ** (np.arange(0, DH, 2, dtype=np.float32) / DH)).astype(np.float32)
    ang = np.arange(P, dtype=np.float32)[:, None] * freqs[None, :]
    sin = np.repeat(np.sin(ang), 2, axis=-1).astype(np.float32)
    cos = np.repeat(np.cos(ang), 2, axis=-1).astype(np.float32)
    sin = np.concatenate([-sin[:, :DH // 2], sin[:, DH // 2:]], axis=-1)
    w1 = np.asarray(inputs["L1_cond_Wqkv"]).reshape(16, 32, 3, D).transpose(3, 2, 0, 1).reshape(D, 3 * D)
    b1 = np.asarray(inputs["L1_cond_bqkv"]).reshape(16, 32, 3).transpose(2, 0, 1).reshape(3, D)
    arrays = {
        "x": x.reshape(B * L, D), "cond": inputs["cond_1024"],
        "w_ada": inputs["L0_cond_W_ada"], "b_ada": inputs["L0_cond_b_ada"],
        "scale1": inputs["L0_cond_scale1"], "scale2": inputs["L0_cond_scale2"],
        "w_qkv0": inputs["L0_cond_W_qkv"], "b_qkv0": inputs["L0_cond_b_qkv"],
        "w_out0": inputs["L0_cond_W_out"], "b_out": inputs["L0_cond_b_out"],
        "w_ff1": inputs["L0_cond_W_ff1"], "b_ff1": inputs["L0_cond_b_ff1"],
        "w_ff2": inputs["L0_cond_W_ff2"], "b_ff2": inputs["L0_cond_b_ff2"],
        "ln_g": inputs["L1_cond_ln_g"], "ln_b": inputs["L1_cond_ln_b"],
        "wg_t": np.asarray(inputs["L1_cond_Wg"]).T, "bg": inputs["L1_cond_bg"],
        "wb_t": np.asarray(inputs["L1_cond_Wb"]).T, "bb": inputs["L1_cond_bb"],
        "w_qkv1": w1, "b_q1": b1[0], "b_k1": b1[1], "b_v1": b1[2],
        "wp_t": np.asarray(inputs["L1_cond_Wp"]).T, "b_p": inputs["L1_cond_bp"],
        "cos": cos, "sin": sin, "ident": np.eye(P, dtype=np.float32),
    }
    arrays = {f"in_{k}": np.ascontiguousarray(v) for k, v in arrays.items()}
    nc = bacc.Bacc("TRN2", target_bir_lowering=False, num_devices=1)
    dram = {k[3:]: nc.dram_tensor(k, list(v.shape), mybir.dt.from_np(v.dtype), kind="ExternalInput").ap()
            for k, v in arrays.items()}
    out = nc.dram_tensor("out", [B * L, D], F32, kind="ExternalOutput").ap()
    build(nc, dram, out)
    r = run_bass_kernel_spmd(nc, [arrays], core_ids=[0])
    return np.asarray(r.results[0]["out"]).reshape(B, L, D)
```
